# Optimizing a Trainium2 kernel written in Bass

```python
import numpy as np
import jax
import jax.numpy as jnp

def _softmax(x, axis=-1):
    return jax.nn.softmax(x, axis=axis)

def _gelu(x):
    return jax.nn.gelu(x, approximate=True)

def _silu(x):
    return jax.nn.silu(x)

def _sigmoid(x):
    return jax.nn.sigmoid(x)

def _layernorm(x, axis=-1, eps=1e-05):
    m = jnp.mean(x, axis=axis, keepdims=True)
    v = jnp.var(x, axis=axis, keepdims=True)
    return (x - m) / jnp.sqrt(v + eps)

def _scatter_add(tgt, idx, src, axis=0):
    return tgt.at[idx].add(src)

def _segment_sum(src, seg, n):
    return jax.ops.segment_sum(src, seg, n)
kernel_name = 'mk_seq_preln_d1_jaxref_r8_fb9bae'

def setup_inputs(seed: int=0):
    np.random.seed(seed)
    _w = jnp.asarray

    def _L0_attn_setup():
        import jax, jax.numpy as jnp
        import numpy as np
        D_MODEL = 128
        NUM_HEADS = 4
        HEAD_QK = 32
        HEAD_V = 64
        EPS = 1e-05
        ROPE_BASE = 10000.0

        def _apply_rotary(q, k):
            T, d = (q.shape[1], q.shape[-1])
            half = d // 2
            inv_freq = 1.0 / ROPE_BASE ** (jnp.arange(0, d, 2, dtype=jnp.float32) / d)
            freqs = jnp.arange(T, dtype=jnp.float32)[:, None] * inv_freq[None, :]
            cos = jnp.cos(freqs)[None, :, None, :]
            sin = jnp.sin(freqs)[None, :, None, :]

            def rot(x):
                x1, x2 = (x[..., :half], x[..., half:])
                return jnp.concatenate([x1 * cos - x2 * sin, x1 * sin + x2 * cos], axis=-1)
            return (rot(q), rot(k))
        key = jax.random.key(seed)
        ks = jax.random.split(key, 7)
        B, T = (2, 256)
        key_dim = NUM_HEADS * HEAD_QK
        value_dim = NUM_HEADS * HEAD_V
        s = 0.02
        return {'x': jax.random.normal(ks[0], (B, T, D_MODEL), jnp.float32), 'Wq': jax.random.normal(ks[1], (key_dim, D_MODEL), jnp.float32) * s, 'Wk': jax.random.normal(ks[2], (key_dim, D_MODEL), jnp.float32) * s, 'Wv': jax.random.normal(ks[3], (value_dim, D_MODEL), jnp.float32) * s, 'Wg': jax.random.normal(ks[4], (value_dim, D_MODEL), jnp.float32) * s, 'Wo': jax.random.normal(ks[5], (D_MODEL, value_dim), jnp.float32) * s, 'g_norm_w': jnp.ones((HEAD_V,), jnp.float32)}
    _L0_attn_in = _L0_attn_setup()

    def _L0_ffn_setup():
        import jax, jax.numpy as jnp
        import numpy as np
        D_MODEL = 128
        HIDDEN = 128
        NUM_EXPERTS = 8
        TOP_K = 2
        key = jax.random.key(seed)
        ks = jax.random.split(key, 10)
        s = 0.02
        return {'x': jax.random.normal(ks[0], (2, 256, D_MODEL), dtype=jnp.float32), 'gate_w': jax.random.normal(ks[1], (NUM_EXPERTS, D_MODEL), dtype=jnp.float32) * s, 'up_w': jax.random.normal(ks[2], (NUM_EXPERTS, D_MODEL, HIDDEN), dtype=jnp.float32) * s, 'up_b': jnp.zeros((NUM_EXPERTS, HIDDEN), dtype=jnp.float32), 'down_w': jax.random.normal(ks[3], (NUM_EXPERTS, HIDDEN, D_MODEL), dtype=jnp.float32) * s, 'down_b': jnp.zeros((NUM_EXPERTS, D_MODEL), dtype=jnp.float32), 'sh_up_w': jax.random.normal(ks[4], (D_MODEL, HIDDEN), dtype=jnp.float32) * s, 'sh_up_b': jnp.zeros((HIDDEN,), dtype=jnp.float32), 'sh_down_w': jax.random.normal(ks[5], (HIDDEN, D_MODEL), dtype=jnp.float32) * s, 'sh_down_b': jnp.zeros((D_MODEL,), dtype=jnp.float32)}
    _L0_ffn_in = _L0_ffn_setup()
    _d = {'L0_attn_x': _L0_attn_in['x'], 'L0_attn_Wq': _L0_attn_in['Wq'], 'L0_attn_Wk': _L0_attn_in['Wk'], 'L0_attn_Wv': _L0_attn_in['Wv'], 'L0_attn_Wg': _L0_attn_in['Wg'], 'L0_attn_Wo': _L0_attn_in['Wo'], 'L0_attn_g_norm_w': _L0_attn_in['g_norm_w'], 'L0_ffn_gate_w': _L0_ffn_in['gate_w'], 'L0_ffn_up_w': _L0_ffn_in['up_w'], 'L0_ffn_up_b': _L0_ffn_in['up_b'], 'L0_ffn_down_w': _L0_ffn_in['down_w'], 'L0_ffn_down_b': _L0_ffn_in['down_b'], 'L0_ffn_sh_up_w': _L0_ffn_in['sh_up_w'], 'L0_ffn_sh_up_b': _L0_ffn_in['sh_up_b'], 'L0_ffn_sh_down_w': _L0_ffn_in['sh_down_w'], 'L0_ffn_sh_down_b': _L0_ffn_in['sh_down_b']}
    _x0 = _d['L0_attn_x']
    _d['L0_attn_x'] = jax.random.normal(jax.random.fold_in(jax.random.key(seed), 1), (2, 1024, 128), dtype=_x0.dtype)
    del _x0
    return _d

def reference(L0_attn_x, L0_attn_Wq, L0_attn_Wk, L0_attn_Wv, L0_attn_Wg, L0_attn_Wo, L0_attn_g_norm_w, L0_ffn_gate_w, L0_ffn_up_w, L0_ffn_up_b, L0_ffn_down_w, L0_ffn_down_b, L0_ffn_sh_up_w, L0_ffn_sh_up_b, L0_ffn_sh_down_w, L0_ffn_sh_down_b):

    def _L0_attn_ref(x, Wq, Wk, Wv, Wg, Wo, g_norm_w):
        import jax, jax.numpy as jnp
        import numpy as np
        D_MODEL = 128
        NUM_HEADS = 4
        HEAD_QK = 32
        HEAD_V = 64
        EPS = 1e-05
        ROPE_BASE = 10000.0

        def _apply_rotary(q, k):
            T, d = (q.shape[1], q.shape[-1])
            half = d // 2
            inv_freq = 1.0 / ROPE_BASE ** (jnp.arange(0, d, 2, dtype=jnp.float32) / d)
            freqs = jnp.arange(T, dtype=jnp.float32)[:, None] * inv_freq[None, :]
            cos = jnp.cos(freqs)[None, :, None, :]
            sin = jnp.sin(freqs)[None, :, None, :]

            def rot(x):
                x1, x2 = (x[..., :half], x[..., half:])
                return jnp.concatenate([x1 * cos - x2 * sin, x1 * sin + x2 * cos], axis=-1)
            return (rot(q), rot(k))
        B, T, _ = x.shape
        H, dk, dv = (NUM_HEADS, HEAD_QK, HEAD_V)
        q = (x @ Wq.T).reshape(B, T, H, dk)
        k = (x @ Wk.T).reshape(B, T, H, dk)
        q, k = _apply_rotary(q, k)
        q = jnp.transpose(q, (0, 2, 1, 3))
        k = jnp.transpose(k, (0, 2, 1, 3))
        v = jnp.transpose((x @ Wv.T).reshape(B, T, H, dv), (0, 2, 1, 3))
        q = q * dk ** (-0.5)
        log_decay = jnp.log1p(-jnp.exp2(-5.0 - jnp.arange(H, dtype=jnp.float32)))
        t = jnp.arange(T, dtype=jnp.float32)
        diff = t[:, None] - t[None, :]
        decay_mask = jnp.where(diff >= 0, jnp.exp(log_decay[:, None, None] * diff[None]), 0.0)
        scores = jnp.einsum('bhtd,bhsd->bhts', q, k) * decay_mask[None]
        o = jnp.einsum('bhts,bhsd->bhtd', scores, v)
        o = jnp.transpose(o, (0, 2, 1, 3))
        rms = jax.lax.rsqrt(jnp.mean(o * o, axis=-1, keepdims=True) + EPS)
        o_n = o * rms * g_norm_w
        g = (x @ Wg.T).reshape(B, T, H, dv)
        o_g = o_n * (g * jax.nn.sigmoid(g))
        return o_g.reshape(B, T, H * dv) @ Wo.T

    def _L0_ffn_ref(x, gate_w, up_w, up_b, down_w, down_b, sh_up_w, sh_up_b, sh_down_w, sh_down_b):
        import jax, jax.numpy as jnp
        import numpy as np
        D_MODEL = 128
        HIDDEN = 128
        NUM_EXPERTS = 8
        TOP_K = 2
        b, s, d = x.shape
        xf = x.reshape(-1, d)
        shared = jax.nn.silu(x @ sh_up_w + sh_up_b) @ sh_down_w + sh_down_b
        logits = xf @ gate_w.T
        scores = jax.nn.softmax(logits, axis=-1)
        topk_w, topk_i = jax.lax.top_k(scores, TOP_K)
        topk_w = topk_w / (topk_w.sum(axis=-1, keepdims=True) + 1e-20)
        comb = (jax.nn.one_hot(topk_i, NUM_EXPERTS, dtype=xf.dtype) * topk_w[..., None]).sum(axis=1)
        h = jnp.einsum('nd,edh->neh', xf, up_w) + up_b
        h = jax.nn.silu(h)
        ye = jnp.einsum('neh,ehd->ned', h, down_w) + down_b
        y = jnp.einsum('ned,ne->nd', ye, comb).reshape(b, s, d)
        return y + shared
    x = L0_attn_x
    x = x + _L0_attn_ref(_layernorm(x, axis=-1), L0_attn_Wq, L0_attn_Wk, L0_attn_Wv, L0_attn_Wg, L0_attn_Wo, L0_attn_g_norm_w)
    x = x + _L0_ffn_ref(_layernorm(x, axis=-1), L0_ffn_gate_w, L0_ffn_up_w, L0_ffn_up_b, L0_ffn_down_w, L0_ffn_down_b, L0_ffn_sh_up_w, L0_ffn_sh_up_b, L0_ffn_sh_down_w, L0_ffn_sh_down_b)
    return x

_drawn_inputs = setup_inputs


def setup_inputs(seed=0):
    import zlib

    import numpy as np

    out = dict(_drawn_inputs(seed))
    spreads = {'L0_attn_g_norm_w': (1.0, 0.6),
     'L0_ffn_up_b': (0.0, 0.8),
     'L0_ffn_down_b': (0.0, 0.1),
     'L0_ffn_sh_up_b': (0.0, 0.656),
     'L0_ffn_sh_down_b': (0.0, 0.1)}
    factors = {'L0_ffn_up_w': 3.109, 'L0_ffn_down_w': 2.874}
    for name, (base, spread) in spreads.items():
        noise = np.random.default_rng([zlib.crc32(name.encode()), seed]).standard_normal(out[name].shape)
        drawn = base * np.exp(spread * noise) if base else spread * noise
        out[name] = jnp.asarray(drawn.astype(out[name].dtype))
    for name, factor in factors.items():
        out[name] = (out[name] * factor).astype(out[name].dtype)
    return out
```

```python
from contextlib import ExitStack

import numpy as np

import concourse.bass as bass
from concourse import mybir

F32 = mybir.dt.float32
F32R = mybir.dt.float32r
ALU = mybir.AluOpType
ACT = mybir.ActivationFunctionType
AX = mybir.AxisListType

P = 128
B = 2
T = 1024
H = 4
DK = 32
DV = 64
HV = H * DV
QK = 2 * H * DK
E = 8
TOP_K = 2
EPS = 1e-5
ROPE_BASE = 10000.0
CHUNKS = T // P
GROUPS = CHUNKS // 2
TILES = 4
GC = TILES * P
GAMMA = [1.0 - 2.0 ** (-5 - h) for h in range(H)]

ROT0 = 0
ROTW = 3 * (DK // 2)
DEC0 = ROT0 + CHUNKS * ROTW
THR0 = DEC0 + 2 * H
GCH0 = THR0 + E * E
NCONST = GCH0 + 1

HI0, LO0, HB0 = 0, 32, 64


def constants():
    half = DK // 2
    inv = (1.0 / np.float32(ROPE_BASE) ** (np.arange(0, DK, 2, dtype=np.float32) / np.float32(DK))).astype(np.float32)
    angle = (np.arange(T, dtype=np.float32)[:, None] * inv[None, :]).astype(np.float64)
    cos, sin = np.cos(angle), np.sin(angle)
    rot = np.concatenate([cos, -sin, sin], axis=1).reshape(CHUNKS, P, ROTW).transpose(1, 0, 2)
    token = np.arange(P, dtype=np.float64)[:, None]
    gamma = np.array(GAMMA)[None, :]
    dec_q = gamma ** (token + 1.0) * DK ** -0.5
    dec_k = gamma ** (P - 1.0 - token)
    i, j = np.arange(E)[:, None], np.arange(E)[None, :]
    thr = np.where(j < i, 0.0, np.where(j > i, float(np.finfo(np.float32).tiny), 1e30))
    gch = np.repeat(np.array(GAMMA) ** P, DK)[:, None]
    return np.concatenate([rot.reshape(P, -1), dec_q, dec_k, np.tile(thr.reshape(1, -1), (P, 1)), gch],
                          axis=1).astype(np.float32)


def later(g):
    return not (isinstance(g, int) and g == 0)


class Signal:

    def __init__(self, sem, per=1):
        self.sem, self.per = sem, per

    def at(self, g, n=1):
        return g * self.per + n


def retention_moe_kernel(nc, x, wqkvg, wot, gnw, upw, upb, dnw, dnb, gatew, const, out):
    ctx = ExitStack()
    with ctx:
        def sb(name, shape, dt=F32):
            return ctx.enter_context(nc.sbuf_tensor(name, shape, dt))

        def bank(name):
            return ctx.enter_context(nc.psum_tensor(name, [P, 512], F32))

        def sig(name, per=1):
            return Signal(ctx.enter_context(nc.semaphore(name)), per)

        X = sb("X", [P, GROUPS * GC])
        W = sb("W", [P, QK + 2 * HV])
        WH = sb("WH", [P, QK + 2 * HV], F32R)
        WL = sb("WL", [P, QK + 2 * HV], F32R)
        WO = sb("WO", [P, 2, P])
        WOG = sb("WOG", [P, 2, P])
        GN = sb("GN", [P, 1])
        UW = sb("UW", [P, (E + 1) * P])
        UWH = sb("UWH", [P, (E + 1) * P], F32R)
        UWL = sb("UWL", [P, (E + 1) * P], F32R)
        UB = sb("UB", [P, E + 1])
        DW = sb("DW", [P, (E + 1) * P])
        DB = sb("DB", [P, P])
        DBX = sb("DBX", [P, P], F32R)
        GW = sb("GW", [P, E])
        GWH = sb("GWH", [P, E], F32R)
        GWL = sb("GWL", [P, E], F32R)
        CN = sb("CN", [P, NCONST])
        COS = sb("COS", [P, CHUNKS * QK])
        SIN = sb("SIN", [P, CHUNKS * QK])
        IDN = sb("IDN", [P, P])
        MASK = sb("MASK", [P, H, P])
        SELF = sb("SELF", [P, E, P])
        SEL = sb("SEL", [P, E, P], F32R)
        NHALF = sb("NHALF", [P, 16])

        ST1 = sb("ST1", [P, 16, 6])
        MV1 = sb("MV1", [P, 16, 2])
        VE1 = sb("VE1", [P, 16])
        RS1 = sb("RS1", [P, 16])
        XN1 = sb("XN1", [P, GC])
        XH1 = sb("XH1", [P, GC], F32R)
        XL1 = sb("XL1", [P, GC], F32R)
        RA = sb("RA", [P, 2, 2, QK])
        RB = sb("RB", [P, 2, 2, QK])
        QKR = sb("QKR", [P, 2, 2, QK])
        V = sb("V", [P, 2, 2, HV])
        SG = sb("SG", [P, 2, 2, HV])
        QT = sb("QT", [P, 2, 2, P])
        KT = sb("KT", [P, 2, 2, P])
        QBD = sb("QBD", [P, 2, 2, H, P])
        SC = sb("SC", [P, TILES, H, P])
        S = sb("S", [P, 2, 2, HV])
        SQ = sb("SQ", [P, 2, 2 * HV])
        SS = sb("SS", [P, 2, 2 * H])
        MS = sb("MS", [P, 2, 2 * H])
        RR = sb("RR", [P, 2, 2 * H])
        SGR = sb("SGR", [P, 2, 2 * HV])
        OG = sb("OG", [P, 2, 2 * HV])
        OGT = sb("OGT", [P, 2, 2, 2, P])
        ST2 = sb("ST2", [P, TILES, 6])
        MV2 = sb("MV2", [P, TILES, 2])
        VE2 = sb("VE2", [P, TILES])
        RS2 = sb("RS2", [P, TILES])
        XN2 = sb("XN2", [P, GC])
        XH2 = sb("XH2", [P, GC], F32R)
        XL2 = sb("XL2", [P, GC], F32R)

        MX = sb("MX", [P, TILES])
        SHI = sb("SHI", [P, TILES, E])
        EX = sb("EX", [P, TILES, E])
        Z = sb("Z", [P, TILES])
        RZ = sb("RZ", [P, TILES])
        PR = sb("PR", [P, TILES, E])
        DIF = sb("DIF", [P, TILES, E, E])
        BEF = sb("BEF", [P, TILES, E, E])
        RANK = sb("RANK", [P, TILES, E])
        WT = sb("WT", [P, TILES, E])
        WS = sb("WS", [P, TILES])
        WSG = sb("WSG", [P, TILES])
        RWS = sb("RWS", [P, TILES])
        CMB = sb("CMB", [P, TILES, E])
        CX = sb("CX", [P, TILES, P])
        CT = sb("CT", [P, GC], F32R)
        HB = sb("HB", [P, 3, GC])
        HG = sb("HG", [P, 2, GC])
        YS = sb("YS", [P, GC])
        OUT = sb("OUT", [P, TILES, P])

        bX = bank("bX")
        bV = bank("bV")
        bS = bank("bS")
        bO = bank("bO")
        bU = [bank("bU0"), bank("bU1")]
        bC = bank("bC")
        bY = bank("bY")

        ld_x = [sig(f"ld_x{g}") for g in range(GROUPS)]
        ld_w, ld_c, ld_wo, ld_gn, ld_up, ld_ub, ld_dn, ld_db, ld_gw = (
            sig(n) for n in ("ld_w", "ld_c", "ld_wo", "ld_gn", "ld_up", "ld_ub", "ld_dn", "ld_db", "ld_gw"))
        db_zero, idn_zero, idn, mask_fill, mask, sel_zero, sel_first, sel_self, sel, nhalf, tables, s_zero, bd_zero, cx_set = (
            sig(n) for n in ("db_zero", "idn_zero", "idn", "mask_fill", "mask", "sel_zero", "sel_first", "sel_self",
                             "sel", "nhalf", "tables", "s_zero", "bd_zero", "cx_set"))
        w_hi, w_lo, uw_hi, uw_lo, gw_hi, gw_lo, wog, db_hi, db_lo = (
            sig(n) for n in ("w_hi", "w_lo", "uw_hi", "uw_lo", "gw_hi", "gw_lo", "wog", "db_hi", "db_lo"))
        ln1_stats, ln1_step, rs1 = sig("ln1_stats"), sig("ln1_step"), sig("rs1")
        xn1, t1, xh1, xl1 = sig("xn1"), sig("t1"), sig("xh1"), sig("xl1")
        qk, v_ps, g_ps, rparts, rot, v_sb, sg = (sig(n, 2) for n in ("qk", "v_ps", "g_ps", "rparts", "rot", "v_sb", "sg"))
        t2, qkt = sig("t2", 2), sig("qkt", 2)
        sc_ps, sc_sb = sig("sc_ps", TILES), sig("sc_sb", TILES)
        kv, st, o_ps, sq, ss, ms, rr, sgr, og = (
            sig(n, 2) for n in ("kv", "st", "o_ps", "sq", "ss", "ms", "rr", "sgr", "og"))
        t3, ogt, wo_ps, x1 = (sig(n, 2) for n in ("t3", "ogt", "wo_ps", "x1"))
        ln2_step = sig("ln2_step", 6)
        rs2, xn2, t4, xh2, xl2 = (sig(n, 2) for n in ("rs2", "xn2", "t4", "xh2", "xl2"))
        logits, exped, comb, ct_ps, ct_sb = (sig(n) for n in ("logits", "exped", "comb", "ct_ps", "ct_sb"))
        route = sig("route", 14)
        up, hid, down = sig("up", E + 1), sig("hid", E + 1), sig("down", E + 1)
        spread, gated = sig("spread", E), sig("gated", E)
        y_sb, yt, outs, stored = sig("y_sb"), sig("yt"), sig("outs"), sig("stored", 32)

        block = ctx.enter_context(nc.Block())

        def product(out_, wide, narrow, start, stop):
            (ah, al), (bh, bl) = wide, narrow
            nc.tensor.matmul(out_, ah, bh, start=start, stop=False)
            nc.tensor.matmul(out_, ah, bl, start=False, stop=False)
            return nc.tensor.matmul(out_, al, bh, start=False, stop=stop)

        def expert(k):
            return E if k == 0 else k - 1

        def cols(t, g, n=GC, off=0):
            return t[:, bass.ds(g * GC + off, n)]

        @block.sync
        def _(sp):
            def load_x(g):
                for b in range(B):
                    dst = X[:, g * GC:(g + 1) * GC].rearrange("r (c b d) -> r b c d", c=2, b=B)[:, b]
                    src = x[b, 2 * g * P:(2 * g + 2) * P, :].rearrange("(c r) d -> r c d", r=P)
                    sp.dma_start(dst, src).then_inc(ld_x[g].sem, 16)

            load_x(0)
            sp.dma_start(CN[:, :], const).then_inc(ld_c.sem, 16)
            for g in range(1, GROUPS):
                load_x(g)
            sp.dma_start(DW[:, :], dnw).then_inc(ld_dn.sem, 16)
            sp.wait_ge(db_zero.sem, 1)
            for r0, n in ((HI0, E + 1), (LO0, E), (HB0, E + 1)):
                sp.dma_start(DB[r0:r0 + n, :], dnb[0:n, :]).then_inc(ld_db.sem, 16)

            def store(g):
                sp.wait_ge(outs.sem, outs.at(g))
                for b in range(B):
                    dst = out[b].rearrange("(g c r) d -> g r c d", c=2, r=P)[g]
                    src = OUT[:, :, :].rearrange("r (c b) d -> r b c d", b=B)[:, b]
                    sp.dma_start(dst, src).then_inc(stored.sem, 16)

            for g in range(GROUPS):
                store(g)
            sp.wait_ge(stored.sem, stored.at(GROUPS - 1, 32))

        @block.gpsimd
        def _(pool):
            pool.memset(NHALF[:, :], -0.5).then_inc(nhalf.sem, 1)
            pool.memset(IDN[:, :], 0.0).then_inc(idn_zero.sem, 1)
            pool.wait_ge(idn_zero.sem, 1)
            pool.affine_select(out=IDN[:, :], in_=IDN[:, :], compare_op=ALU.not_equal, fill=1.0, base=0,
                               pattern=[[-1, P]], channel_multiplier=1).then_inc(idn.sem, 1)
            def rstd1(n0, n1, step):
                pool.wait_ge(nhalf.sem, 1)
                pool.wait_ge(ln1_step.sem, step)
                pool.tensor_tensor(RS1[:, n0:n1], VE1[:, n0:n1], NHALF[:, 0:n1 - n0], ALU.pow).then_inc(rs1.sem, 1)

            def table(c):
                dec = CN[:, DEC0:DEC0 + 2 * H]
                r0 = ROT0 + c * ROTW
                half = DK // 2
                cos = CN[:, r0:r0 + half]
                sin = CN[:, r0 + half:r0 + ROTW]
                pool.tensor_tensor(
                    COS[:, c * QK:(c + 1) * QK].rearrange("r (h a f) -> r h a f", a=2, f=half),
                    cos.unsqueeze(1).unsqueeze(1).to_broadcast([P, 2 * H, 2, half]),
                    dec.unsqueeze(2).unsqueeze(2).to_broadcast([P, 2 * H, 2, half]), ALU.mult)
                pool.tensor_tensor(
                    SIN[:, c * QK:(c + 1) * QK].rearrange("r (h f) -> r h f", f=DK),
                    sin.unsqueeze(1).to_broadcast([P, 2 * H, DK]),
                    dec.unsqueeze(2).to_broadcast([P, 2 * H, DK]), ALU.mult).then_inc(tables.sem, 1)

            pool.wait_ge(ld_c.sem, 16)
            table(0)
            rstd1(0, TILES, 1)
            for h in range(H):
                last = pool.memset(MASK[:, h, :], GAMMA[h] ** -P)
            last.then_inc(mask_fill.sem, 1)
            pool.wait_ge(mask_fill.sem, 1)
            pool.affine_select(out=MASK[:, :, :], in_=MASK[:, :, :], compare_op=ALU.is_ge, fill=0.0, base=0,
                               pattern=[[0, H], [1, P]], channel_multiplier=-1).then_inc(mask.sem, 1)

            def rotate(g, p):
                pool.wait_ge(rparts.sem, rparts.at(g, p + 1))
                if later(g):
                    pool.wait_ge(kv.sem, kv.at(g - 1, p + 1))
                pool.tensor_tensor(QKR[:, p].rearrange("r b n -> r (b n)"), RA[:, p].rearrange("r b n -> r (b n)"),
                                   RB[:, p].rearrange("r b n -> r (b n)"), ALU.add).then_inc(rot.sem, 1)

            def rms(g, p):
                pool.wait_ge(ms.sem, ms.at(g, p + 1))
                pool.tensor_tensor(RR[:, p], MS[:, p], NHALF[:, 0:2 * H], ALU.pow).then_inc(rr.sem, 1)
                pool.wait_ge(rr.sem, rr.at(g, p + 1))
                pool.wait_ge(sg.sem, sg.at(g, p + 1))
                pool.tensor_tensor(SGR[:, p].rearrange("r (h v) -> r h v", v=DV),
                                   SG[:, p].rearrange("r b (h v) -> r (b h) v", v=DV),
                                   RR[:, p].unsqueeze(2).to_broadcast([P, 2 * H, DV]), ALU.mult).then_inc(sgr.sem, 1)

            def rstd2(g, p):
                pool.wait_ge(ln2_step.sem, ln2_step.at(g, 3 * p + 3))
                pool.tensor_tensor(RS2[:, 2 * p:2 * p + 2], VE2[:, 2 * p:2 * p + 2], NHALF[:, 0:2],
                                   ALU.pow).then_inc(rs2.sem, 1)

            def attention(g):
                rotate(g, 0)
                rotate(g, 1)
                rms(g, 0)
                rstd2(g, 0)
                rms(g, 1)
                rstd2(g, 1)

            table(1)
            rotate(0, 0)
            rstd1(TILES, 16, 2)
            pool.memset(SELF[:, :, :], 0.0).then_inc(sel_zero.sem, 1)
            pool.wait_ge(sel_zero.sem, 1)
            pool.affine_select(out=SELF[:, :, :], in_=SELF[:, :, :], compare_op=ALU.not_equal, fill=1.0, base=-HI0,
                               pattern=[[-1, E], [0, P]], channel_multiplier=1).then_inc(sel_first.sem, 1)
            rotate(0, 1)
            pool.wait_ge(sel_first.sem, 1)
            pool.affine_select(out=SELF[:, :, :], in_=SELF[:, :, :], compare_op=ALU.not_equal, fill=1.0, base=-LO0,
                               pattern=[[-1, E], [0, P]], channel_multiplier=1).then_inc(sel_self.sem, 1)
            rms(0, 0)
            for c in range(2, 5):
                table(c)
            rstd2(0, 0)
            rms(0, 1)
            for c in range(5, CHUNKS):
                table(c)
            rstd2(0, 1)
            for g in range(1, GROUPS):
                attention(g)

        @block.scalar
        def _(act):
            act.dma_start(W[:, :], wqkvg).then_inc(ld_w.sem, 16)
            act.dma_start(WO[:, :, :], wot).then_inc(ld_wo.sem, 16)
            act.dma_start(GN[:, :], gnw).then_inc(ld_gn.sem, 16)
            act.dma_start(GW[:, :], gatew).then_inc(ld_gw.sem, 16)
            act.dma_start(UB[:, :], upb).then_inc(ld_ub.sem, 16)
            act.dma_start(UW[:, :], upw).then_inc(ld_up.sem, 16)
            act.wait_ge(ld_w.sem, 16)
            act.copy(WH[:, :], W[:, :]).then_inc(w_hi.sem, 1)

            def x1_hi(g):
                act.wait_ge(t1.sem, t1.at(g))
                if later(g):
                    act.wait_ge(g_ps.sem, g_ps.at(g - 1, 2))
                act.copy(XH1[:, :], bX[:, :]).then_inc(xh1.sem, 1)

            def values(g, p):
                act.wait_ge(v_ps.sem, v_ps.at(g, p + 1))
                if later(g):
                    act.wait_ge(kv.sem, kv.at(g - 1, p + 1))
                    act.wait_ge(o_ps.sem, o_ps.at(g - 1, p + 1))
                act.copy(V[:, p].rearrange("r b n -> r (b n)"), bV[:, :]).then_inc(v_sb.sem, 1)

            def gates(g, p):
                act.wait_ge(g_ps.sem, g_ps.at(g, p + 1))
                if later(g):
                    act.wait_ge(sgr.sem, sgr.at(g - 1, p + 1))
                act.activation(SG[:, p].rearrange("r b n -> r (b n)"), bV[:, :], ACT.Silu).then_inc(sg.sem, 1)

            def transposed_qk(g, p):
                act.wait_ge(t2.sem, t2.at(g, p + 1))
                if later(g):
                    act.wait_ge(o_ps.sem, o_ps.at(g - 1, p + 1))
                elif p == 0:
                    act.wait_ge(bd_zero.sem, 1)
                act.copy(KT[:, p].rearrange("r b n -> r (b n)"), bX[:, 2 * P:4 * P])
                for h in range(H):
                    r = slice(h * DK, (h + 1) * DK)
                    act.copy(QBD[r, p, :, h, :], bX[r, 0:2 * P].rearrange("r (b n) -> r b n", b=2))
                act.copy(QT[:, p].rearrange("r b n -> r (b n)"), bX[:, 0:2 * P]).then_inc(qkt.sem, 1)

            def squares(g, p):
                act.wait_ge(o_ps.sem, o_ps.at(g, p + 1))
                if later(g):
                    act.wait_ge(ss.sem, ss.at(g - 1, p + 1))
                act.activation(SQ[:, p], bO[:, :], ACT.Square).then_inc(sq.sem, 1)

            def transposed_out(g, p):
                act.wait_ge(t3.sem, t3.at(g, p + 1))
                if later(g):
                    act.wait_ge(wo_ps.sem, wo_ps.at(g - 1, p + 1))
                act.copy(OGT[:, p].rearrange("r b a n -> r (b a n)"), bV[:, :]).then_inc(ogt.sem, 1)

            def x2_hi(g, p):
                act.wait_ge(t4.sem, t4.at(g, p + 1))
                if later(g):
                    act.wait_ge(up.sem, up.at(g - 1, E + 1))
                act.copy(XH2[:, p * 2 * P:(p + 1) * 2 * P], bV[:, 0:2 * P]).then_inc(xh2.sem, 1)

            def hidden(g, k):
                e = expert(k)
                act.wait_ge(up.sem, up.at(g, k + 1))
                if k >= 4:
                    act.wait_ge(gated.sem, gated.at(g, k - 3))
                elif k == 3:
                    act.wait_ge(down.sem, down.at(g, 1))
                elif later(g):
                    act.wait_ge(gated.sem, gated.at(g - 1, k + 6))
                act.activation(HB[:, k % 3, :], bU[k % 2][:, :], ACT.Silu, bias=UB[:, e:e + 1]).then_inc(hid.sem, 1)

            def exps(g):
                act.wait_ge(route.sem, route.at(g, 2))
                act.activation(EX[:, :, :], SHI[:, :, :], ACT.Exp).then_inc(exped.sem, 1)

            def comb_t(g):
                act.wait_ge(ct_ps.sem, ct_ps.at(g))
                if later(g):
                    act.wait_ge(down.sem, down.at(g - 1, E + 1))
                act.copy(CT[:, :], bC[:, :]).then_inc(ct_sb.sem, 1)

            def sums(g):
                act.wait_ge(down.sem, down.at(g, E + 1))
                if later(g):
                    act.wait_ge(yt.sem, yt.at(g - 1))
                act.copy(YS[:, :], bY[:, :]).then_inc(y_sb.sem, 1)

            x1_hi(0)
            act.wait_ge(ld_gw.sem, 16)
            act.copy(GWH[:, :], GW[:, :]).then_inc(gw_hi.sem, 1)
            values(0, 0)
            gates(0, 0)
            transposed_qk(0, 0)
            values(0, 1)
            gates(0, 1)
            act.wait_ge(ld_up.sem, 16)
            act.copy(UWH[:, :], UW[:, :]).then_inc(uw_hi.sem, 1)
            transposed_qk(0, 1)
            act.wait_ge(ld_db.sem, 48)
            act.copy(DBX[0:HB0, :], DB[0:HB0, :])
            act.copy(CT[HB0:P, 0:P], DB[HB0:P, :]).then_inc(db_hi.sem, 1)
            squares(0, 0)
            transposed_out(0, 0)
            squares(0, 1)
            x2_hi(0, 0)
            transposed_out(0, 1)
            x2_hi(0, 1)
            act.wait_ge(ld_ub.sem, 16)
            act.wait_ge(db_lo.sem, 1)

            def steady(g):
                f = g - 1
                hidden(f, 0)
                x1_hi(g)
                hidden(f, 1)
                values(g, 0)
                gates(g, 0)
                exps(f)
                transposed_qk(g, 0)
                comb_t(f)
                values(g, 1)
                gates(g, 1)
                hidden(f, 2)
                hidden(f, 3)
                transposed_qk(g, 1)
                squares(g, 0)
                hidden(f, 4)
                transposed_out(g, 0)
                hidden(f, 5)
                squares(g, 1)
                hidden(f, 6)
                hidden(f, 7)
                x2_hi(g, 0)
                hidden(f, 8)
                transposed_out(g, 1)
                x2_hi(g, 1)
                sums(f)

            for g in range(1, GROUPS):
                steady(g)
            f = GROUPS - 1
            hidden(f, 0)
            hidden(f, 1)
            exps(f)
            comb_t(f)
            for k in range(2, E + 1):
                hidden(f, k)
            sums(f)

        @block.vector
        def _(dve):
            dve.memset(DB[:, :], 0.0).then_inc(db_zero.sem, 1)
            dve.memset(QBD[:, 0], 0.0)
            dve.memset(QBD[:, 1], 0.0).then_inc(bd_zero.sem, 1)
            dve.memset(S[:, :, :, :], 0.0).then_inc(s_zero.sem, 1)
            dve.memset(CX[:, :, :], 0.0).then_inc(cx_set.sem, 1)
            dve.wait_ge(cx_set.sem, 1)
            dve.memset(CX[:, :, HI0 + E:HI0 + E + 1], 1.0)
            dve.memset(CX[:, :, HB0 + E:HB0 + E + 1], 1.0).then_inc(cx_set.sem, 1)

            def stats1(t0, t1_, step):
                for t in range(t0, t1_):
                    last = dve.bn_stats(ST1[:, t, :], X[:, t * P:(t + 1) * P])
                last.then_inc(ln1_stats.sem, 1)
                dve.wait_ge(ln1_stats.sem, 2 * step - 1)
                for t in range(t0, t1_):
                    last = dve.bn_aggr(MV1[:, t, :], ST1[:, t, :])
                last.then_inc(ln1_stats.sem, 1)
                dve.wait_ge(ln1_stats.sem, 2 * step)
                dve.tensor_scalar(VE1[:, t0:t1_], MV1[:, t0:t1_, 1], EPS, None, ALU.add).then_inc(ln1_step.sem, 1)

            def normalize1(g):
                dve.wait_ge(rs1.sem, 1 if not later(g) else 2)
                if later(g):
                    dve.wait_ge(t1.sem, t1.at(g - 1))
                for m in range(TILES):
                    mean = MV1.rearrange("r t s -> r (t s)")[:, bass.ds(g * 2 * TILES + 2 * m, 1)]
                    rstd = RS1[:, bass.ds(g * TILES + m, 1)]
                    last = dve.tensor_scalar(XN1[:, m * P:(m + 1) * P], cols(X, g, P, m * P), mean, rstd,
                                             ALU.subtract, ALU.mult)
                last.then_inc(xn1.sem, 1)

            def x1_lo(g):
                dve.wait_ge(xh1.sem, xh1.at(g))
                dve.tensor_tensor(XL1[:, :], bX[:, :], XH1[:, :].bitcast(F32), ALU.subtract).then_inc(xl1.sem, 1)

            def rotary(g, p):
                dve.wait_ge(qk.sem, qk.at(g, p + 1))
                if isinstance(g, int):
                    dve.wait_ge(tables.sem, 2 * g + p + 1)
                else:
                    dve.wait_ge(tables.sem, CHUNKS)
                if later(g):
                    dve.wait_ge(rot.sem, rot.at(g - 1, p + 1))
                cos = COS[:, bass.ds(g * 2 * QK + p * QK, QK)]
                sin = SIN[:, bass.ds(g * 2 * QK + p * QK, QK)]
                half = DK // 2
                src = bX[:, :].rearrange("r (b n) -> r b n", b=2)
                dve.tensor_tensor(RA[:, p], src, cos.unsqueeze(1).to_broadcast([P, 2, QK]), ALU.mult)
                for b in range(2):
                    sw = bX[:, b * QK:(b + 1) * QK].rearrange("r (h a f) -> r h a f", a=2, f=half)[:, :, ::-1, :]
                    last = dve.tensor_tensor(RB[:, p, b].rearrange("r (h a f) -> r h a f", a=2, f=half), sw,
                                             sin.rearrange("r (h a f) -> r h a f", a=2, f=half), ALU.mult)
                last.then_inc(rparts.sem, 1)

            def masked(g, m):
                dve.wait_ge(sc_ps.sem, sc_ps.at(g, m + 1))
                if later(g):
                    dve.wait_ge(o_ps.sem, o_ps.at(g - 1, m // 2 + 1))
                elif m == 0:
                    dve.wait_ge(mask.sem, 1)
                dve.tensor_tensor(SC[:, m].rearrange("r h n -> r (h n)"), bS[:, :],
                                  MASK[:, :, :].rearrange("r h n -> r (h n)"), ALU.mult).then_inc(sc_sb.sem, 1)

            def state(g, p):
                dve.wait_ge(kv.sem, kv.at(g, p + 1))
                if p == 1:
                    dve.wait_ge(o_ps.sem, o_ps.at(g, 1))
                elif later(g):
                    dve.wait_ge(o_ps.sem, o_ps.at(g - 1, 2))
                if p == 1:
                    dve.wait_ge(st.sem, st.at(g, 1))
                elif later(g):
                    dve.wait_ge(st.sem, st.at(g - 1, 2))
                else:
                    dve.wait_ge(s_zero.sem, 1)
                for h in range(H):
                    r, c = slice(h * DK, (h + 1) * DK), slice(h * DV, (h + 1) * DV)
                    last = dve.scalar_tensor_tensor(
                        out=S[r, 1 - p, :, c], in0=S[r, p, :, c], scalar=CN[r, GCH0:GCH0 + 1],
                        in1=bS[r, :].rearrange("r (b n) -> r b n", b=2)[:, :, c], op0=ALU.mult, op1=ALU.add)
                last.then_inc(st.sem, 1)

            def mean_squares(g, p):
                dve.wait_ge(sq.sem, sq.at(g, p + 1))
                dve.tensor_reduce(SS[:, p], SQ[:, p].rearrange("r (h v) -> r h v", v=DV), AX.X, ALU.add).then_inc(ss.sem, 1)
                dve.wait_ge(ss.sem, ss.at(g, p + 1))
                dve.tensor_scalar(MS[:, p], SS[:, p], 1.0 / DV, EPS, ALU.mult, ALU.add).then_inc(ms.sem, 1)

            def gate_out(g, p):
                dve.wait_ge(sgr.sem, sgr.at(g, p + 1))
                if later(g):
                    dve.wait_ge(t3.sem, t3.at(g - 1, p + 1))
                dve.tensor_tensor(OG[:, p], bO[:, :], SGR[:, p], ALU.mult).then_inc(og.sem, 1)

            def add_attention(g, p):
                dve.wait_ge(wo_ps.sem, wo_ps.at(g, p + 1))
                xs = cols(X, g, 2 * P, p * 2 * P)
                dve.tensor_tensor(xs, bV[:, 0:2 * P], xs, ALU.add).then_inc(x1.sem, 1)

            def stats2(g, p):
                dve.wait_ge(x1.sem, x1.at(g, p + 1))
                for m in (2 * p, 2 * p + 1):
                    last = dve.bn_stats(ST2[:, m, :], cols(X, g, P, m * P))
                last.then_inc(ln2_step.sem, 1)
                dve.wait_ge(ln2_step.sem, ln2_step.at(g, 3 * p + 1))
                for m in (2 * p, 2 * p + 1):
                    last = dve.bn_aggr(MV2[:, m, :], ST2[:, m, :])
                last.then_inc(ln2_step.sem, 1)
                dve.wait_ge(ln2_step.sem, ln2_step.at(g, 3 * p + 2))
                dve.tensor_scalar(VE2[:, 2 * p:2 * p + 2], MV2[:, 2 * p:2 * p + 2, 1], EPS, None,
                                  ALU.add).then_inc(ln2_step.sem, 1)

            def normalize2(g, p):
                dve.wait_ge(rs2.sem, rs2.at(g, p + 1))
                for m in (2 * p, 2 * p + 1):
                    last = dve.tensor_scalar(XN2[:, m * P:(m + 1) * P], cols(X, g, P, m * P), MV2[:, m, 0:1],
                                             RS2[:, m:m + 1], ALU.subtract, ALU.mult)
                last.then_inc(xn2.sem, 1)

            def x2_lo(g, p):
                dve.wait_ge(xh2.sem, xh2.at(g, p + 1))
                c = slice(p * 2 * P, (p + 1) * 2 * P)
                dve.tensor_tensor(XL2[:, c], bV[:, 0:2 * P], XH2[:, c].bitcast(F32), ALU.subtract).then_inc(xl2.sem, 1)

            def route_a(g):
                lg = bC[:, 0:TILES * E].rearrange("r (m e) -> r m e", e=E)
                dve.wait_ge(logits.sem, logits.at(g))
                dve.tensor_reduce(MX[:, :], lg, AX.X, ALU.max).then_inc(route.sem, 1)
                dve.wait_ge(route.sem, route.at(g, 1))
                dve.tensor_tensor(SHI[:, :, :], lg, MX[:, :].unsqueeze(2).to_broadcast([P, TILES, E]),
                                  ALU.subtract).then_inc(route.sem, 1)

            def route_b(g):
                wide = [P, TILES, E, E]
                step = [2]

                def then(ins):
                    step[0] += 1
                    ins.then_inc(route.sem, 1)
                    dve.wait_ge(route.sem, route.at(g, step[0]))

                dve.wait_ge(exped.sem, exped.at(g))
                then(dve.tensor_reduce(Z[:, :], EX[:, :, :], AX.X, ALU.add))
                then(dve.reciprocal(RZ[:, :], Z[:, :]))
                then(dve.tensor_tensor(PR[:, :, :], EX[:, :, :], RZ[:, :].unsqueeze(2).to_broadcast([P, TILES, E]), ALU.mult))
                then(dve.tensor_tensor(DIF[:, :, :, :], PR[:, :, :].unsqueeze(2).to_broadcast(wide),
                                       PR[:, :, :].unsqueeze(3).to_broadcast(wide), ALU.subtract))
                thr = CN[:, THR0:THR0 + E * E].unsqueeze(1).to_broadcast([P, TILES, E * E])
                then(dve.tensor_tensor(BEF[:, :, :, :].rearrange("r m i j -> r m (i j)"),
                                       DIF[:, :, :, :].rearrange("r m i j -> r m (i j)"), thr, ALU.is_ge))
                then(dve.tensor_reduce(RANK[:, :, :], BEF[:, :, :, :], AX.X, ALU.add))
                then(dve.scalar_tensor_tensor(out=WT[:, :, :], in0=RANK[:, :, :], scalar=float(TOP_K), in1=PR[:, :, :],
                                              op0=ALU.is_lt, op1=ALU.mult))
                then(dve.tensor_reduce(WS[:, :], WT[:, :, :], AX.X, ALU.add))
                then(dve.tensor_scalar(WSG[:, :], WS[:, :], 1e-20, None, ALU.add))
                then(dve.reciprocal(RWS[:, :], WSG[:, :]))
                then(dve.tensor_tensor(CMB[:, :, :], WT[:, :, :], RWS[:, :].unsqueeze(2).to_broadcast([P, TILES, E]), ALU.mult))
                if later(g):
                    dve.wait_ge(ct_ps.sem, ct_ps.at(g - 1))
                hi = CX[:, :, HI0:HI0 + E].bitcast(F32R)
                dve.tensor_copy(CX[:, :, HB0:HB0 + E].bitcast(F32R), CMB[:, :, :])
                then(dve.tensor_copy(hi, CMB[:, :, :]))
                dve.tensor_tensor(CX[:, :, LO0:LO0 + E], CMB[:, :, :], CX[:, :, HI0:HI0 + E],
                                  ALU.subtract).then_inc(comb.sem, 1)

            def gating(g, k):
                dve.wait_ge(spread.sem, spread.at(g, k))
                dve.wait_ge(hid.sem, hid.at(g, k + 1))
                if k >= 3:
                    dve.wait_ge(down.sem, down.at(g, k - 1))
                elif later(g):
                    dve.wait_ge(down.sem, down.at(g - 1, k + 7))
                dve.tensor_tensor(HG[:, k % 2, :], bC[:, :], HB[:, k % 3, :], ALU.mult).then_inc(gated.sem, 1)

            def result(g):
                dve.wait_ge(yt.sem, yt.at(g))
                if later(g):
                    dve.wait_ge(stored.sem, stored.at(g - 1, 32))
                dve.tensor_tensor(OUT[:, :, :].rearrange("r m n -> r (m n)"), bY[:, :], cols(X, g),
                                  ALU.add).then_inc(outs.sem, 1)

            dve.wait_ge(ld_x[0].sem, 32)
            stats1(0, TILES, 1)
            dve.wait_ge(w_hi.sem, 1)
            dve.tensor_tensor(WL[:, :], W[:, :], WH[:, :].bitcast(F32), ALU.subtract).then_inc(w_lo.sem, 1)
            normalize1(0)
            x1_lo(0)
            rotary(0, 0)
            for g in range(1, GROUPS):
                dve.wait_ge(ld_x[g].sem, 32)
            stats1(TILES, 16, 2)
            masked(0, 0)
            rotary(0, 1)
            masked(0, 1)
            state(0, 0)
            masked(0, 2)
            masked(0, 3)
            state(0, 1)
            dve.wait_ge(ld_wo.sem, 16)
            dve.wait_ge(ld_gn.sem, 16)
            dve.tensor_scalar(WOG[:, :, :].rearrange("r a n -> r (a n)"), WO[:, :, :].rearrange("r a n -> r (a n)"),
                              GN[:, 0:1], None, ALU.mult).then_inc(wog.sem, 1)
            mean_squares(0, 0)
            dve.wait_ge(uw_hi.sem, 1)
            dve.tensor_tensor(UWL[:, :], UW[:, :], UWH[:, :].bitcast(F32), ALU.subtract).then_inc(uw_lo.sem, 1)
            gate_out(0, 0)
            dve.wait_ge(gw_hi.sem, 1)
            dve.tensor_tensor(GWL[:, :], GW[:, :], GWH[:, :].bitcast(F32), ALU.subtract).then_inc(gw_lo.sem, 1)
            dve.wait_ge(db_hi.sem, 1)
            dve.tensor_tensor(DBX[HB0:P, :], DB[HB0:P, :], CT[HB0:P, 0:P].bitcast(F32), ALU.subtract).then_inc(db_lo.sem, 1)
            dve.wait_ge(sel_self.sem, 1)
            dve.tensor_copy(SEL[:, :, :], SELF[:, :, :]).then_inc(sel.sem, 1)
            add_attention(0, 0)
            stats2(0, 0)
            mean_squares(0, 1)
            gate_out(0, 1)
            normalize2(0, 0)
            x2_lo(0, 0)
            add_attention(0, 1)
            stats2(0, 1)
            normalize2(0, 1)
            x2_lo(0, 1)

            def steady(g):
                f = g - 1
                normalize1(g)
                route_a(f)
                x1_lo(g)
                rotary(g, 0)
                route_b(f)
                masked(g, 0)
                masked(g, 1)
                rotary(g, 1)
                gating(f, 1)
                gating(f, 2)
                state(g, 0)
                masked(g, 2)
                gating(f, 3)
                masked(g, 3)
                state(g, 1)
                mean_squares(g, 0)
                gating(f, 4)
                gate_out(g, 0)
                gating(f, 5)
                mean_squares(g, 1)
                add_attention(g, 0)
                stats2(g, 0)
                gating(f, 6)
                gate_out(g, 1)
                normalize2(g, 0)
                gating(f, 7)
                x2_lo(g, 0)
                add_attention(g, 1)
                stats2(g, 1)
                gating(f, 8)
                normalize2(g, 1)
                x2_lo(g, 1)
                result(f)

            for g in range(1, GROUPS):
                steady(g)
            f = GROUPS - 1
            route_a(f)
            route_b(f)
            for k in range(1, E + 1):
                gating(f, k)
            result(f)

        @block.tensor
        def _(pe):
            def x1_t(g):
                pe.wait_ge(xn1.sem, xn1.at(g))
                if later(g):
                    pe.wait_ge(qkt.sem, qkt.at(g - 1, 2))
                else:
                    pe.wait_ge(idn.sem, 1)
                for m in range(TILES):
                    last = pe.transpose(bX[:, m * P:(m + 1) * P], XN1[:, m * P:(m + 1) * P], IDN[:, :])
                last.then_inc(t1.sem, 1)

            def project(g, p, dst, c0, n, done):
                for b in range(2):
                    m = 2 * p + b
                    t = slice(m * P, (m + 1) * P)
                    last = product(dst[:, b * n:(b + 1) * n], (XH1[:, t], XL1[:, t]),
                                   (WH[:, c0:c0 + n], WL[:, c0:c0 + n]), True, True)
                last.then_inc(done.sem, 1)

            def proj_qk(g, p):
                if p == 0:
                    pe.wait_ge(xl1.sem, xl1.at(g))
                    if not later(g):
                        pe.wait_ge(w_lo.sem, 1)
                else:
                    pe.wait_ge(qkt.sem, qkt.at(g, 1))
                project(g, p, bX, 0, QK, qk)

            def proj_v(g, p):
                if p == 0:
                    if later(g):
                        pe.wait_ge(xl2.sem, xl2.at(g - 1, 2))
                else:
                    pe.wait_ge(sg.sem, sg.at(g, 1))
                project(g, p, bV, QK, HV, v_ps)

            def proj_g(g, p):
                pe.wait_ge(v_sb.sem, v_sb.at(g, p + 1))
                project(g, p, bV, QK + HV, HV, g_ps)

            def qk_t(g, p):
                pe.wait_ge(rot.sem, rot.at(g, p + 1))
                for a in range(2):
                    for b in range(2):
                        o = (2 * a + b) * P
                        last = pe.transpose(bX[:, o:o + P], QKR[:, p, b, a * P:(a + 1) * P], IDN[:, :])
                last.then_inc(t2.sem, 1)

            def scores(g, m):
                p, b = divmod(m, 2)
                if b == 0:
                    pe.wait_ge(qkt.sem, qkt.at(g, p + 1))
                if m in (1, 3):
                    pe.wait_ge(sc_sb.sem, sc_sb.at(g, m))
                elif m == 2:
                    pe.wait_ge(st.sem, st.at(g, 1))
                elif later(g):
                    pe.wait_ge(st.sem, st.at(g - 1, 2))
                pe.matmul(bS[:, :], KT[:, p, b, :], QBD[:, p, b].rearrange("r h n -> r (h n)"), start=True,
                          stop=True).then_inc(sc_ps.sem, 1)

            def state_add(g, p):
                pe.wait_ge(sc_sb.sem, sc_sb.at(g, 2 * p + 2))
                pe.wait_ge(v_sb.sem, v_sb.at(g, p + 1))
                for b in range(2):
                    last = pe.matmul(bS[:, b * HV:(b + 1) * HV], QKR[:, p, b, P:2 * P], V[:, p, b, :],
                                     start=True, stop=True)
                last.then_inc(kv.sem, 1)

            def attend(g, p):
                if p == 1:
                    pe.wait_ge(og.sem, og.at(g, 1))
                    pe.wait_ge(st.sem, st.at(g, 1))
                elif later(g):
                    pe.wait_ge(og.sem, og.at(g - 1, 2))
                    pe.wait_ge(st.sem, st.at(g - 1, 2))
                else:
                    pe.wait_ge(s_zero.sem, 1)
                pe.wait_ge(sc_sb.sem, sc_sb.at(g, 2 * p + 2))
                for b in range(2):
                    pe.matmul(bO[:, b * HV:(b + 1) * HV], QT[:, p, b, :], S[:, p, b, :], start=True, stop=False)
                    for h in range(H):
                        c = slice(b * HV + h * DV, b * HV + (h + 1) * DV)
                        last = pe.matmul(bO[:, c], SC[:, 2 * p + b, h, :], V[:, p, b, h * DV:(h + 1) * DV],
                                         start=False, stop=(h == H - 1))
                last.then_inc(o_ps.sem, 1)

            def out_t(g, p):
                pe.wait_ge(og.sem, og.at(g, p + 1))
                if p == 0:
                    pe.wait_ge(sg.sem, sg.at(g, 2))
                else:
                    pe.wait_ge(xl2.sem, xl2.at(g, 1))
                for b in range(2):
                    for a in range(2):
                        o = (2 * b + a) * P
                        last = pe.transpose(bV[:, o:o + P], OG[:, p, o:o + P], IDN[:, :])
                last.then_inc(t3.sem, 1)

            def proj_out(g, p):
                pe.wait_ge(ogt.sem, ogt.at(g, p + 1))
                if not later(g):
                    pe.wait_ge(wog.sem, 1)
                for b in range(2):
                    for a in range(2):
                        last = pe.matmul(bV[:, b * P:(b + 1) * P], OGT[:, p, b, a, :], WOG[:, a, :],
                                         start=(a == 0), stop=(a == 1))
                last.then_inc(wo_ps.sem, 1)

            def x2_t(g, p):
                pe.wait_ge(xn2.sem, xn2.at(g, p + 1))
                for b in range(2):
                    m = 2 * p + b
                    last = pe.transpose(bV[:, b * P:(b + 1) * P], XN2[:, m * P:(m + 1) * P], IDN[:, :])
                last.then_inc(t4.sem, 1)

            def router(g):
                pe.wait_ge(xl2.sem, xl2.at(g, 2))
                if not later(g):
                    pe.wait_ge(gw_lo.sem, 1)
                else:
                    pe.wait_ge(gated.sem, gated.at(g - 1, E))
                for m in range(TILES):
                    t = slice(m * P, (m + 1) * P)
                    last = product(bC[:, m * E:(m + 1) * E], (XH2[:, t], XL2[:, t]), (GWH[:, :], GWL[:, :]), True, True)
                last.then_inc(logits.sem, 1)

            def comb_t(g):
                pe.wait_ge(comb.sem, comb.at(g))
                for m in range(TILES):
                    last = pe.transpose(bC[:, m * P:(m + 1) * P], CX[:, m, :], IDN[:, :])
                last.then_inc(ct_ps.sem, 1)

            def up_proj(g, k):
                e = expert(k)
                if k == 0:
                    pe.wait_ge(xl2.sem, xl2.at(g, 2))
                    if not later(g):
                        pe.wait_ge(uw_lo.sem, 1)
                if k >= 2:
                    pe.wait_ge(hid.sem, hid.at(g, k - 1))
                elif later(g):
                    pe.wait_ge(hid.sem, hid.at(g - 1, E + 1 - k))
                w = slice(e * P, (e + 1) * P)
                product(bU[k % 2][:, :], (UWH[:, w], UWL[:, w]), (XH2[:, :], XL2[:, :]), True, True).then_inc(up.sem, 1)

            def spread_comb(g, k):
                if k == 1:
                    pe.wait_ge(ct_sb.sem, ct_sb.at(g))
                    if not later(g):
                        pe.wait_ge(sel.sem, 1)
                else:
                    pe.wait_ge(gated.sem, gated.at(g, k - 1))
                pe.matmul(bC[:, :], SEL[:, expert(k), :], CT[:, :], start=True, stop=True).then_inc(spread.sem, 1)

            def down_proj(g, k):
                e = expert(k)
                if k == 0:
                    pe.wait_ge(hid.sem, hid.at(g, 1))
                    if later(g):
                        pe.wait_ge(outs.sem, outs.at(g - 1))
                    else:
                        pe.wait_ge(ld_dn.sem, 16)
                else:
                    pe.wait_ge(gated.sem, gated.at(g, k))
                if k == E:
                    pe.matmul(bY[:, :], DBX[:, :], CT[:, :], start=False, stop=False)
                rhs = HB[:, 0, :] if k == 0 else HG[:, k % 2, :]
                pe.matmul(bY[:, :], DW[:, e * P:(e + 1) * P], rhs, start=(k == 0), stop=(k == E)).then_inc(down.sem, 1)

            def y_t(g):
                pe.wait_ge(y_sb.sem, y_sb.at(g))
                for m in range(TILES):
                    last = pe.transpose(bY[:, m * P:(m + 1) * P], YS[:, m * P:(m + 1) * P], IDN[:, :])
                last.then_inc(yt.sem, 1)

            x1_t(0)
            proj_qk(0, 0)
            proj_v(0, 0)
            proj_g(0, 0)
            qk_t(0, 0)
            proj_v(0, 1)
            proj_qk(0, 1)
            proj_g(0, 1)
            scores(0, 0)
            scores(0, 1)
            state_add(0, 0)
            attend(0, 0)
            qk_t(0, 1)
            scores(0, 2)
            scores(0, 3)
            state_add(0, 1)
            out_t(0, 0)
            attend(0, 1)
            proj_out(0, 0)
            x2_t(0, 0)
            out_t(0, 1)
            proj_out(0, 1)
            x2_t(0, 1)

            def steady(g):
                f = g - 1
                router(f)
                up_proj(f, 0)
                x1_t(g)
                up_proj(f, 1)
                proj_qk(g, 0)
                proj_v(g, 0)
                down_proj(f, 0)
                proj_g(g, 0)
                qk_t(g, 0)
                comb_t(f)
                proj_v(g, 1)
                proj_qk(g, 1)
                proj_g(g, 1)
                up_proj(f, 2)
                scores(g, 0)
                spread_comb(f, 1)
                scores(g, 1)
                up_proj(f, 3)
                spread_comb(f, 2)
                state_add(g, 0)
                down_proj(f, 1)
                qk_t(g, 1)
                attend(g, 0)
                down_proj(f, 2)
                scores(g, 2)
                spread_comb(f, 3)
                up_proj(f, 4)
                scores(g, 3)
                down_proj(f, 3)
                state_add(g, 1)
                spread_comb(f, 4)
                up_proj(f, 5)
                out_t(g, 0)
                down_proj(f, 4)
                attend(g, 1)
                proj_out(g, 0)
                spread_comb(f, 5)
                up_proj(f, 6)
                down_proj(f, 5)
                spread_comb(f, 6)
                x2_t(g, 0)
                up_proj(f, 7)
                down_proj(f, 6)
                spread_comb(f, 7)
                up_proj(f, 8)
                out_t(g, 1)
                down_proj(f, 7)
                proj_out(g, 1)
                spread_comb(f, 8)
                down_proj(f, 8)
                x2_t(g, 1)
                y_t(f)

            for g in range(1, GROUPS):
                steady(g)
            f = GROUPS - 1
            router(f)
            up_proj(f, 0)
            up_proj(f, 1)
            down_proj(f, 0)
            up_proj(f, 2)
            comb_t(f)
            spread_comb(f, 1)
            for k in range(1, E + 1):
                if k + 2 <= E:
                    up_proj(f, k + 2)
                if k + 1 <= E:
                    spread_comb(f, k + 1)
                down_proj(f, k)
            y_t(f)


def kernel(**inputs):
    import concourse.bacc as bacc
    from concourse.bass_utils import run_bass_kernel_spmd

    def arr(name):
        return np.asarray(inputs[name])

    both = np.concatenate
    feeds = {
        "x": arr("L0_attn_x"),
        "wqkvg": both([arr("L0_attn_" + n) for n in ("Wq", "Wk", "Wv", "Wg")], axis=0).T,
        "wot": arr("L0_attn_Wo").T.reshape(2, P, P).transpose(1, 0, 2),
        "gnw": np.tile(arr("L0_attn_g_norm_w"), P // DV)[:, None],
        "upw": both([arr("L0_ffn_up_w"), arr("L0_ffn_sh_up_w")[None]]).transpose(1, 0, 2).reshape(P, -1),
        "upb": both([arr("L0_ffn_up_b"), arr("L0_ffn_sh_up_b")[None]]).T,
        "dnw": both([arr("L0_ffn_down_w"), arr("L0_ffn_sh_down_w")[None]]).transpose(1, 0, 2).reshape(P, -1),
        "dnb": both([arr("L0_ffn_down_b"), arr("L0_ffn_sh_down_b")[None]]),
        "gatew": arr("L0_ffn_gate_w").T,
        "const": constants(),
    }
    feeds = {name: np.ascontiguousarray(a) for name, a in feeds.items()}
    nc = bacc.Bacc("TRN2", target_bir_lowering=False, num_devices=1)
    args = [nc.dram_tensor(name, a.shape, mybir.dt.from_np(a.dtype), kind="ExternalInput").ap()
            for name, a in feeds.items()]
    args.append(nc.dram_tensor("out", (B, T, P), F32, kind="ExternalOutput").ap())
    retention_moe_kernel(nc, *args)
    done = run_bass_kernel_spmd(nc, [feeds], core_ids=[0])
    return done.results[0]["out"]
```

```python
from contextlib import ExitStack

import numpy as np

import concourse.bass as bass
from concourse import mybir

F32 = mybir.dt.float32
F32R = mybir.dt.float32r
ALU = mybir.AluOpType
ACT = mybir.ActivationFunctionType
AX = mybir.AxisListType

P = 128
B = 2
T = 1024
H = 4
DK = 32
DV = 64
HV = H * DV
QK = 2 * H * DK
E = 8
TOP_K = 2
EPS = 1e-5
ROPE_BASE = 10000.0
CHUNKS = T // P
GROUPS = CHUNKS // 2
TILES = 4
GC = TILES * P
GAMMA = [1.0 - 2.0 ** (-5 - h) for h in range(H)]

ROT0 = 0
ROTW = 3 * (DK // 2)
DEC0 = ROT0 + CHUNKS * ROTW
THR0 = DEC0 + 2 * H
GCH0 = THR0 + E * E
NCONST = GCH0 + 1

HI0, LO0, HB0 = 0, 32, 64


def constants():
    half = DK // 2
    inv = (1.0 / np.float32(ROPE_BASE) ** (np.arange(0, DK, 2, dtype=np.float32) / np.float32(DK))).astype(np.float32)
    angle = (np.arange(T, dtype=np.float32)[:, None] * inv[None, :]).astype(np.float64)
    cos, sin = np.cos(angle), np.sin(angle)
    rot = np.concatenate([cos, -sin, sin], axis=1).reshape(CHUNKS, P, ROTW).transpose(1, 0, 2)
    token = np.arange(P, dtype=np.float64)[:, None]
    gamma = np.array(GAMMA)[None, :]
    dec_q = gamma ** (token + 1.0) * DK ** -0.5
    dec_k = gamma ** (P - 1.0 - token)
    i, j = np.arange(E)[:, None], np.arange(E)[None, :]
    thr = np.where(j < i, 0.0, np.where(j > i, float(np.finfo(np.float32).tiny), 1e30))
    gch = np.repeat(np.array(GAMMA) ** P, DK)[:, None]
    return np.concatenate([rot.reshape(P, -1), dec_q, dec_k, np.tile(thr.reshape(1, -1), (P, 1)), gch],
                          axis=1).astype(np.float32)


def later(g):
    return not (isinstance(g, int) and g == 0)


class Signal:

    def __init__(self, sem, per=1):
        self.sem, self.per = sem, per

    def at(self, g, n=1):
        return g * self.per + n


def retention_moe_kernel(nc, x, wqkvg, wot, gnw, upw, upb, dnw, dnb, gatew, const, out):
    ctx = ExitStack()
    with ctx:
        def sb(name, shape, dt=F32):
            return ctx.enter_context(nc.sbuf_tensor(name, shape, dt))

        def bank(name):
            return ctx.enter_context(nc.psum_tensor(name, [P, 512], F32))

        def sig(name, per=1):
            return Signal(ctx.enter_context(nc.semaphore(name)), per)

        X = sb("X", [P, GROUPS * GC])
        W = sb("W", [P, QK + 2 * HV])
        WH = sb("WH", [P, QK + 2 * HV], F32R)
        WL = sb("WL", [P, QK + 2 * HV], F32R)
        WO = sb("WO", [P, 2, P])
        WOG = sb("WOG", [P, 2, P])
        GN = sb("GN", [P, 1])
        UW = sb("UW", [P, (E + 1) * P])
        UWH = sb("UWH", [P, (E + 1) * P], F32R)
        UWL = sb("UWL", [P, (E + 1) * P], F32R)
        UB = sb("UB", [P, E + 1])
        DW = sb("DW", [P, (E + 1) * P])
        DWH = sb("DWH", [P, (E + 1) * P], F32R)
        DWL = sb("DWL", [P, (E + 1) * P], F32R)
        DB = sb("DB", [P, P])
        DBX = sb("DBX", [P, P], F32R)
        GW = sb("GW", [P, E])
        GWH = sb("GWH", [P, E], F32R)
        GWL = sb("GWL", [P, E], F32R)
        CN = sb("CN", [P, NCONST])
        COS = sb("COS", [P, CHUNKS * QK])
        SIN = sb("SIN", [P, CHUNKS * QK])
        IDN = sb("IDN", [P, P])
        MASK = sb("MASK", [P, H, P])
        SELF = sb("SELF", [P, E, P])
        SEL = sb("SEL", [P, E, P], F32R)
        NHALF = sb("NHALF", [P, 16])

        WARM = sb("WARM", [P, 1])

        ST1 = sb("ST1", [P, 16, 6])
        MV1 = sb("MV1", [P, 16, 2])
        VE1 = sb("VE1", [P, 16])
        RS1 = sb("RS1", [P, 16])
        XN1 = sb("XN1", [P, GC])
        XH1 = sb("XH1", [P, GC], F32R)
        XL1 = sb("XL1", [P, GC], F32R)
        RA = sb("RA", [P, 2, 2, QK])
        RB = sb("RB", [P, 2, 2, QK])
        QKR = sb("QKR", [P, 2, 2, QK])
        V = sb("V", [P, 2, 2, HV])
        SG = sb("SG", [P, 2, 2, HV])
        QT = sb("QT", [P, 2, 2, P])
        KT = sb("KT", [P, 2, 2, P])
        QBD = sb("QBD", [P, 2, 2, H, P])
        SC = sb("SC", [P, TILES, H, P])
        S = sb("S", [P, 2, 2, HV])
        SQ = sb("SQ", [P, 2, 2 * HV])
        SS = sb("SS", [P, 2, 2 * H])
        MS = sb("MS", [P, 2, 2 * H])
        RR = sb("RR", [P, 2, 2 * H])
        OGR = sb("OGR", [P, 2, 2 * HV])
        OG = sb("OG", [P, 2, 2 * HV])
        OGT = sb("OGT", [P, 2, 2, 2, P])
        ST2 = sb("ST2", [P, TILES, 6])
        MV2 = sb("MV2", [P, TILES, 2])
        VE2 = sb("VE2", [P, TILES])
        RS2 = sb("RS2", [P, TILES])
        XN2 = sb("XN2", [P, GC])
        XH2 = sb("XH2", [P, GC], F32R)
        XL2 = sb("XL2", [P, GC], F32R)

        MX = sb("MX", [P, TILES])
        SHI = sb("SHI", [P, TILES, E])
        EX = sb("EX", [P, TILES, E])
        Z = sb("Z", [P, TILES])
        RZ = sb("RZ", [P, TILES])
        PR = sb("PR", [P, TILES, E])
        DIF = sb("DIF", [P, TILES, E, E])
        BEF = sb("BEF", [P, TILES, E, E])
        RANK = sb("RANK", [P, TILES, E])
        WT = sb("WT", [P, TILES, E])
        WS = sb("WS", [P, TILES])
        WSG = sb("WSG", [P, TILES])
        RWS = sb("RWS", [P, TILES])
        CMB = sb("CMB", [P, TILES, E])
        CX = sb("CX", [P, TILES, P])
        CT = sb("CT", [P, GC], F32R)
        HB = sb("HB", [P, 3, GC])
        HG = sb("HG", [P, 3, GC])
        HGH = sb("HGH", [P, 3, GC], F32R)
        HGL = sb("HGL", [P, 3, GC], F32R)
        YS = sb("YS", [P, GC])
        OUT = sb("OUT", [P, TILES, P])

        bX = bank("bX")
        bV = bank("bV")
        bS = bank("bS")
        bO = bank("bO")
        bU = [bank("bU0"), bank("bU1")]
        bC = bank("bC")
        bY = bank("bY")

        ld_x = [sig(f"ld_x{g}") for g in range(GROUPS)]
        ld_w, ld_c, ld_wo, ld_gn, ld_up, ld_ub, ld_dn, ld_db, ld_gw = (
            sig(n) for n in ("ld_w", "ld_c", "ld_wo", "ld_gn", "ld_up", "ld_ub", "ld_dn", "ld_db", "ld_gw"))
        db_zero, idn_zero, idn, mask_fill, mask, sel_zero, sel_first, sel_self, sel, nhalf, warm, tables, s_zero, bd_zero, cx_set = (
            sig(n) for n in ("db_zero", "idn_zero", "idn", "mask_fill", "mask", "sel_zero", "sel_first", "sel_self",
                             "sel", "nhalf", "warm", "tables", "s_zero", "bd_zero", "cx_set"))
        w_hi, w_lo, uw_hi, uw_lo, dw_hi, dw_lo, gw_hi, gw_lo, wog, db_hi, db_lo = (
            sig(n) for n in ("w_hi", "w_lo", "uw_hi", "uw_lo", "dw_hi", "dw_lo", "gw_hi", "gw_lo", "wog", "db_hi", "db_lo"))
        ln1_stats, ln1_step, rs1 = sig("ln1_stats"), sig("ln1_step"), sig("rs1")
        xn1, t1, xh1, xl1 = sig("xn1"), sig("t1"), sig("xh1"), sig("xl1")
        qk, v_ps, g_ps, rparts, rot, v_sb, sg = (sig(n, 2) for n in ("qk", "v_ps", "g_ps", "rparts", "rot", "v_sb", "sg"))
        t2, kt, qt = sig("t2", 2), sig("kt", 2), sig("qt", 2)
        sc_ps, sc_sb = sig("sc_ps", TILES), sig("sc_sb", TILES)
        kv, st, o_ps, sq, ss, ms, rr, ogr, og = (
            sig(n, 2) for n in ("kv", "st", "o_ps", "sq", "ss", "ms", "rr", "ogr", "og"))
        t3, ogt, wo_ps, x1 = (sig(n, 2) for n in ("t3", "ogt", "wo_ps", "x1"))
        ln2_step = sig("ln2_step", 6)
        rs2, xn2, t4, xh2, xl2 = (sig(n, 2) for n in ("rs2", "xn2", "t4", "xh2", "xl2"))
        logits, exped, comb, ct_ps, ct_sb = (sig(n) for n in ("logits", "exped", "comb", "ct_ps", "ct_sb"))
        route = sig("route", 14)
        up, hid, down = sig("up", E + 1), sig("hid", E + 1), sig("down", E + 1)
        spread, gated = sig("spread", E), sig("gated", E)
        hg_hi, hg_lo = sig("hg_hi", E + 1), sig("hg_lo", E + 1)
        y_sb, yt, outs, stored = sig("y_sb"), sig("yt"), sig("outs"), sig("stored", 32)

        block = ctx.enter_context(nc.Block())

        def product(out_, wide, narrow, start, stop):
            (ah, al), (bh, bl) = wide, narrow
            nc.tensor.matmul(out_, ah, bh, start=start, stop=False)
            nc.tensor.matmul(out_, ah, bl, start=False, stop=False)
            return nc.tensor.matmul(out_, al, bh, start=False, stop=stop)

        def expert(k):
            return E if k == 0 else k - 1

        def cols(t, g, n=GC, off=0):
            return t[:, bass.ds(g * GC + off, n)]

        @block.sync
        def _(sp):
            def load_x(g):
                for b in range(B):
                    dst = X[:, g * GC:(g + 1) * GC].rearrange("r (c b d) -> r b c d", c=2, b=B)[:, b]
                    src = x[b, 2 * g * P:(2 * g + 2) * P, :].rearrange("(c r) d -> r c d", r=P)
                    sp.dma_start(dst, src).then_inc(ld_x[g].sem, 16)

            load_x(0)
            sp.dma_start(CN[:, :], const).then_inc(ld_c.sem, 16)
            for g in range(1, GROUPS):
                load_x(g)
            sp.dma_start(DW[:, :], dnw).then_inc(ld_dn.sem, 16)
            sp.wait_ge(db_zero.sem, 1)
            for r0, n in ((HI0, E + 1), (LO0, E), (HB0, E + 1)):
                sp.dma_start(DB[r0:r0 + n, :], dnb[0:n, :]).then_inc(ld_db.sem, 16)

            def store(g):
                sp.wait_ge(outs.sem, outs.at(g))
                for b in range(B):
                    dst = out[b].rearrange("(g c r) d -> g r c d", c=2, r=P)[g]
                    src = OUT[:, :, :].rearrange("r (c b) d -> r b c d", b=B)[:, b]
                    sp.dma_start(dst, src).then_inc(stored.sem, 16)

            for g in range(GROUPS):
                store(g)
            sp.wait_ge(stored.sem, stored.at(GROUPS - 1, 32))

        @block.gpsimd
        def _(pool):
            pool.memset(NHALF[:, :], -0.5).then_inc(nhalf.sem, 1)
            pool.memset(IDN[:, :], 0.0).then_inc(idn_zero.sem, 1)
            pool.wait_ge(idn_zero.sem, 1)
            pool.affine_select(out=IDN[:, :], in_=IDN[:, :], compare_op=ALU.not_equal, fill=1.0, base=0,
                               pattern=[[-1, P]], channel_multiplier=1).then_inc(idn.sem, 1)
            pool.memset(QBD[:, 0], 0.0)
            pool.memset(QBD[:, 1], 0.0).then_inc(bd_zero.sem, 1)
            pool.memset(S[:, :, :, :], 0.0).then_inc(s_zero.sem, 1)
            def rstd1(n0, n1, step):
                pool.wait_ge(nhalf.sem, 1)
                pool.wait_ge(ln1_step.sem, step)
                pool.tensor_tensor(RS1[:, n0:n1], VE1[:, n0:n1], NHALF[:, 0:n1 - n0], ALU.pow).then_inc(rs1.sem, 1)

            def tables_of(*chunks):
                pool.wait_ge(ld_c.sem, 16)
                for c in chunks:
                    table(c)

            def table(c):
                dec = CN[:, DEC0:DEC0 + 2 * H]
                r0 = ROT0 + c * ROTW
                half = DK // 2
                cos = CN[:, r0:r0 + half]
                sin = CN[:, r0 + half:r0 + ROTW]
                pool.tensor_tensor(
                    COS[:, c * QK:(c + 1) * QK].rearrange("r (h a f) -> r h a f", a=2, f=half),
                    cos.unsqueeze(1).unsqueeze(1).to_broadcast([P, 2 * H, 2, half]),
                    dec.unsqueeze(2).unsqueeze(2).to_broadcast([P, 2 * H, 2, half]), ALU.mult)
                pool.tensor_tensor(
                    SIN[:, c * QK:(c + 1) * QK].rearrange("r (h f) -> r h f", f=DK),
                    sin.unsqueeze(1).to_broadcast([P, 2 * H, DK]),
                    dec.unsqueeze(2).to_broadcast([P, 2 * H, DK]), ALU.mult).then_inc(tables.sem, 1)

            def causal_mask():
                for h in range(H):
                    last = pool.memset(MASK[:, h, :], GAMMA[h] ** -P)
                last.then_inc(mask_fill.sem, 1)
                pool.wait_ge(mask_fill.sem, 1)
                pool.affine_select(out=MASK[:, :, :], in_=MASK[:, :, :], compare_op=ALU.is_ge, fill=0.0, base=0,
                                   pattern=[[0, H], [1, P]], channel_multiplier=-1).then_inc(mask.sem, 1)

            def rms(g, p):
                pool.wait_ge(ms.sem, ms.at(g, p + 1))
                pool.tensor_tensor(RR[:, p], MS[:, p], NHALF[:, 0:2 * H], ALU.pow).then_inc(rr.sem, 1)

            def normalize_out(g, p):
                pool.wait_ge(rr.sem, rr.at(g, p + 1))
                pool.wait_ge(ogr.sem, ogr.at(g, p + 1))
                if later(g):
                    pool.wait_ge(t3.sem, t3.at(g - 1, p + 1))
                pool.tensor_tensor(OG[:, p].rearrange("r (h v) -> r h v", v=DV),
                                   OGR[:, p].rearrange("r (h v) -> r h v", v=DV),
                                   RR[:, p].unsqueeze(2).to_broadcast([P, 2 * H, DV]), ALU.mult).then_inc(og.sem, 1)

            def gated_lo(g, k):
                pool.wait_ge(hg_hi.sem, hg_hi.at(g, k + 1))
                pool.tensor_tensor(HGL[:, k % 3, :], HB[:, 0, :] if k == 0 else HG[:, k % 3, :],
                                   HGH[:, k % 3, :].bitcast(F32), ALU.subtract).then_inc(hg_lo.sem, 1)

            def rstd2(g, p):
                pool.wait_ge(ln2_step.sem, ln2_step.at(g, 3 * p + 3))
                pool.tensor_tensor(RS2[:, 2 * p:2 * p + 2], VE2[:, 2 * p:2 * p + 2], NHALF[:, 0:2],
                                   ALU.pow).then_inc(rs2.sem, 1)

            def selector():
                pool.memset(SELF[:, :, :], 0.0).then_inc(sel_zero.sem, 1)
                pool.wait_ge(sel_zero.sem, 1)
                pool.affine_select(out=SELF[:, :, :], in_=SELF[:, :, :], compare_op=ALU.not_equal, fill=1.0, base=-HI0,
                                   pattern=[[-1, E], [0, P]], channel_multiplier=1).then_inc(sel_first.sem, 1)
                pool.wait_ge(sel_first.sem, 1)
                pool.affine_select(out=SELF[:, :, :], in_=SELF[:, :, :], compare_op=ALU.not_equal, fill=1.0, base=-LO0,
                                   pattern=[[-1, E], [0, P]], channel_multiplier=1).then_inc(sel_self.sem, 1)

            rstd1(0, TILES, 1)
            tables_of(0)
            tables_of(1)
            causal_mask()
            tables_of(*range(2, CHUNKS))
            rstd1(TILES, GROUPS * TILES, 2)
            selector()
            rms(0, 0)
            normalize_out(0, 0)
            rstd2(0, 0)
            rms(0, 1)
            normalize_out(0, 1)
            rstd2(0, 1)

            def steady(g):
                f = g - 1
                gated_lo(f, 0)
                rms(g, 0)
                normalize_out(g, 0)
                gated_lo(f, 1)
                gated_lo(f, 2)
                gated_lo(f, 3)
                rstd2(g, 0)
                rms(g, 1)
                gated_lo(f, 4)
                gated_lo(f, 5)
                normalize_out(g, 1)
                gated_lo(f, 6)
                gated_lo(f, 7)
                gated_lo(f, 8)
                rstd2(g, 1)

            for g in range(1, GROUPS):
                steady(g)
            f = GROUPS - 1
            gated_lo(f, 0)
            gated_lo(f, 1)
            gated_lo(f, 2)
            gated_lo(f, 3)
            gated_lo(f, 4)
            gated_lo(f, 5)
            gated_lo(f, 6)
            gated_lo(f, 7)
            gated_lo(f, 8)

        @block.scalar
        def _(act):
            act.wait_ge(nhalf.sem, 1)
            act.activation(WARM[:, :], NHALF[:, 0:1], ACT.Silu).then_inc(warm.sem, 1)
            act.dma_start(W[:, :], wqkvg).then_inc(ld_w.sem, 16)
            act.dma_start(WO[:, :, :], wot).then_inc(ld_wo.sem, 16)
            act.dma_start(GN[:, :], gnw).then_inc(ld_gn.sem, 16)
            act.dma_start(GW[:, :], gatew).then_inc(ld_gw.sem, 16)
            act.dma_start(UB[:, :], upb).then_inc(ld_ub.sem, 16)
            act.dma_start(UW[:, :], upw).then_inc(ld_up.sem, 16)

            def x1_hi(g):
                act.wait_ge(t1.sem, t1.at(g))
                if later(g):
                    act.wait_ge(qk.sem, qk.at(g - 1, 2))
                    act.wait_ge(g_ps.sem, g_ps.at(g - 1, 2))
                act.copy(XH1[:, :], bX[:, :]).then_inc(xh1.sem, 1)

            def values(g, p):
                act.wait_ge(v_ps.sem, v_ps.at(g, p + 1))
                if later(g):
                    act.wait_ge(kv.sem, kv.at(g - 1, p + 1))
                    act.wait_ge(o_ps.sem, o_ps.at(g - 1, p + 1))
                act.copy(V[:, p].rearrange("r b n -> r (b n)"), bV[:, :]).then_inc(v_sb.sem, 1)

            def gates(g, p):
                act.wait_ge(g_ps.sem, g_ps.at(g, p + 1))
                if later(g):
                    act.wait_ge(ogr.sem, ogr.at(g - 1, p + 1))
                act.activation(SG[:, p].rearrange("r b n -> r (b n)"), bV[:, :], ACT.Silu).then_inc(sg.sem, 1)

            def keys_t(g, p):
                act.wait_ge(t2.sem, t2.at(g, p + 1))
                if later(g):
                    act.wait_ge(o_ps.sem, o_ps.at(g - 1, p + 1))
                elif p == 0:
                    act.wait_ge(bd_zero.sem, 1)
                act.copy(KT[:, p].rearrange("r b n -> r (b n)"), bX[:, 2 * P:4 * P])
                for h in range(H):
                    r = slice(h * DK, (h + 1) * DK)
                    last = act.copy(QBD[r, p, :, h, :], bX[r, 0:2 * P].rearrange("r (b n) -> r b n", b=2))
                last.then_inc(kt.sem, 1)

            def queries_t(g, p):
                act.wait_ge(t2.sem, t2.at(g, p + 1))
                if later(g):
                    act.wait_ge(o_ps.sem, o_ps.at(g - 1, p + 1))
                act.copy(QT[:, p].rearrange("r b n -> r (b n)"), bX[:, 0:2 * P]).then_inc(qt.sem, 1)

            def squares(g, p):
                act.wait_ge(o_ps.sem, o_ps.at(g, p + 1))
                if later(g):
                    act.wait_ge(ss.sem, ss.at(g - 1, p + 1))
                act.activation(SQ[:, p], bO[:, :], ACT.Square).then_inc(sq.sem, 1)

            def transposed_out(g, p):
                act.wait_ge(t3.sem, t3.at(g, p + 1))
                if later(g):
                    act.wait_ge(wo_ps.sem, wo_ps.at(g - 1, p + 1))
                act.copy(OGT[:, p].rearrange("r b a n -> r (b a n)"), bV[:, :]).then_inc(ogt.sem, 1)

            def x2_hi(g, p):
                act.wait_ge(t4.sem, t4.at(g, p + 1))
                if later(g):
                    act.wait_ge(up.sem, up.at(g - 1, E + 1))
                act.copy(XH2[:, p * 2 * P:(p + 1) * 2 * P], bV[:, 0:2 * P]).then_inc(xh2.sem, 1)

            def hidden(g, k):
                e = expert(k)
                act.wait_ge(up.sem, up.at(g, k + 1))
                if k >= 4:
                    act.wait_ge(gated.sem, gated.at(g, k - 3))
                elif k == 3:
                    act.wait_ge(hg_lo.sem, hg_lo.at(g, 1))
                elif later(g):
                    act.wait_ge(gated.sem, gated.at(g - 1, k + 6))
                if k == 0 and not later(g):
                    act.wait_ge(ld_ub.sem, 16)
                act.activation(HB[:, k % 3, :], bU[k % 2][:, :], ACT.Silu, bias=UB[:, e:e + 1]).then_inc(hid.sem, 1)

            def gated_hi(g, k):
                if k == 0:
                    act.wait_ge(hid.sem, hid.at(g, 1))
                else:
                    act.wait_ge(gated.sem, gated.at(g, k))
                if k >= 3:
                    act.wait_ge(down.sem, down.at(g, k - 2))
                elif later(g):
                    act.wait_ge(down.sem, down.at(g - 1, k + 7))
                act.copy(HGH[:, k % 3, :], HB[:, 0, :] if k == 0 else HG[:, k % 3, :]).then_inc(hg_hi.sem, 1)

            def exps(g):
                act.wait_ge(route.sem, route.at(g, 2))
                act.activation(EX[:, :, :], SHI[:, :, :], ACT.Exp).then_inc(exped.sem, 1)

            def comb_sb(g):
                act.wait_ge(ct_ps.sem, ct_ps.at(g))
                if later(g):
                    act.wait_ge(down.sem, down.at(g - 1, E + 1))
                else:
                    act.wait_ge(db_lo.sem, 1)
                act.copy(CT[:, :], bC[:, :]).then_inc(ct_sb.sem, 1)

            def sums(g):
                act.wait_ge(down.sem, down.at(g, E + 1))
                if later(g):
                    act.wait_ge(yt.sem, yt.at(g - 1))
                act.copy(YS[:, :], bY[:, :]).then_inc(y_sb.sem, 1)

            def split_w():
                act.wait_ge(ld_w.sem, 16)
                act.copy(WH[:, :], W[:, :]).then_inc(w_hi.sem, 1)

            def split_experts():
                act.wait_ge(ld_gw.sem, 16)
                act.copy(GWH[:, :], GW[:, :]).then_inc(gw_hi.sem, 1)
                act.wait_ge(ld_up.sem, 16)
                act.copy(UWH[:, :], UW[:, :]).then_inc(uw_hi.sem, 1)
                act.wait_ge(ld_db.sem, 48)
                act.copy(DBX[0:HB0, :], DB[0:HB0, :])
                act.copy(CT[HB0:P, 0:P], DB[HB0:P, :]).then_inc(db_hi.sem, 1)

            def split_down():
                act.wait_ge(ld_dn.sem, 16)
                act.copy(DWH[:, :], DW[:, :]).then_inc(dw_hi.sem, 1)

            split_w()
            x1_hi(0)
            split_experts()
            keys_t(0, 0)
            values(0, 0)
            queries_t(0, 0)
            gates(0, 0)
            values(0, 1)
            split_down()
            squares(0, 0)
            keys_t(0, 1)
            gates(0, 1)
            transposed_out(0, 0)
            queries_t(0, 1)
            squares(0, 1)
            x1_hi(1)
            x2_hi(0, 0)
            transposed_out(0, 1)
            x2_hi(0, 1)

            def steady(g):
                f = g - 1
                keys_t(g, 0)
                queries_t(g, 0)
                values(g, 0)
                exps(f)
                hidden(f, 0)
                gates(g, 0)
                hidden(f, 1)
                gated_hi(f, 0)
                keys_t(g, 1)
                squares(g, 0)
                comb_sb(f)
                values(g, 1)
                queries_t(g, 1)
                hidden(f, 2)
                gated_hi(f, 1)
                gates(g, 1)
                hidden(f, 3)
                transposed_out(g, 0)
                gated_hi(f, 2)
                gated_hi(f, 3)
                squares(g, 1)
                hidden(f, 4)
                if g + 1 < GROUPS:
                    x1_hi(g + 1)
                hidden(f, 5)
                gated_hi(f, 4)
                hidden(f, 6)
                gated_hi(f, 5)
                hidden(f, 7)
                hidden(f, 8)
                x2_hi(g, 0)
                gated_hi(f, 6)
                gated_hi(f, 7)
                transposed_out(g, 1)
                gated_hi(f, 8)
                sums(f)
                x2_hi(g, 1)

            for g in range(1, GROUPS):
                steady(g)
            f = GROUPS - 1
            exps(f)
            hidden(f, 0)
            gated_hi(f, 0)
            hidden(f, 1)
            comb_sb(f)
            hidden(f, 2)
            hidden(f, 3)
            gated_hi(f, 1)
            gated_hi(f, 2)
            hidden(f, 4)
            gated_hi(f, 3)
            hidden(f, 5)
            hidden(f, 6)
            gated_hi(f, 4)
            gated_hi(f, 5)
            hidden(f, 7)
            gated_hi(f, 6)
            hidden(f, 8)
            gated_hi(f, 7)
            gated_hi(f, 8)
            sums(f)

        @block.vector
        def _(dve):
            dve.memset(DB[:, :], 0.0).then_inc(db_zero.sem, 1)
            dve.memset(CX[:, :, :], 0.0).then_inc(cx_set.sem, 1)
            dve.wait_ge(cx_set.sem, 1)
            dve.memset(CX[:, :, HI0 + E:HI0 + E + 1], 1.0)
            dve.memset(CX[:, :, HB0 + E:HB0 + E + 1], 1.0).then_inc(cx_set.sem, 1)

            def stats1(t0, t1_, step):
                for t in range(t0, t1_):
                    last = dve.bn_stats(ST1[:, t, :], X[:, t * P:(t + 1) * P])
                last.then_inc(ln1_stats.sem, 1)
                dve.wait_ge(ln1_stats.sem, 2 * step - 1)
                for t in range(t0, t1_):
                    last = dve.bn_aggr(MV1[:, t, :], ST1[:, t, :])
                last.then_inc(ln1_stats.sem, 1)
                dve.wait_ge(ln1_stats.sem, 2 * step)
                dve.tensor_scalar(VE1[:, t0:t1_], MV1[:, t0:t1_, 1], EPS, None, ALU.add).then_inc(ln1_step.sem, 1)

            def normalize1(g):
                dve.wait_ge(rs1.sem, 1 if not later(g) else 2)
                if later(g):
                    dve.wait_ge(t1.sem, t1.at(g - 1))
                for m in range(TILES):
                    mean = MV1.rearrange("r t s -> r (t s)")[:, bass.ds(g * 2 * TILES + 2 * m, 1)]
                    rstd = RS1[:, bass.ds(g * TILES + m, 1)]
                    last = dve.tensor_scalar(XN1[:, m * P:(m + 1) * P], cols(X, g, P, m * P), mean, rstd,
                                             ALU.subtract, ALU.mult)
                last.then_inc(xn1.sem, 1)

            def x1_lo(g):
                dve.wait_ge(xh1.sem, xh1.at(g))
                dve.tensor_tensor(XL1[:, :], bX[:, :], XH1[:, :].bitcast(F32), ALU.subtract).then_inc(xl1.sem, 1)

            def rotary(g, p):
                dve.wait_ge(qk.sem, qk.at(g, p + 1))
                if isinstance(g, int):
                    dve.wait_ge(tables.sem, 2 * g + p + 1)
                else:
                    dve.wait_ge(tables.sem, CHUNKS)
                if later(g):
                    dve.wait_ge(rot.sem, rot.at(g - 1, p + 1))
                cos = COS[:, bass.ds(g * 2 * QK + p * QK, QK)]
                sin = SIN[:, bass.ds(g * 2 * QK + p * QK, QK)]
                half = DK // 2
                src = bX[:, :].rearrange("r (b n) -> r b n", b=2)
                dve.tensor_tensor(RA[:, p], src, cos.unsqueeze(1).to_broadcast([P, 2, QK]), ALU.mult)
                for b in range(2):
                    sw = bX[:, b * QK:(b + 1) * QK].rearrange("r (h a f) -> r h a f", a=2, f=half)[:, :, ::-1, :]
                    last = dve.tensor_tensor(RB[:, p, b].rearrange("r (h a f) -> r h a f", a=2, f=half), sw,
                                             sin.rearrange("r (h a f) -> r h a f", a=2, f=half), ALU.mult)
                last.then_inc(rparts.sem, 1)

            def rotate(g, p):
                dve.wait_ge(rparts.sem, rparts.at(g, p + 1))
                if later(g):
                    dve.wait_ge(kv.sem, kv.at(g - 1, p + 1))
                dve.tensor_tensor(QKR[:, p].rearrange("r b n -> r (b n)"), RA[:, p].rearrange("r b n -> r (b n)"),
                                  RB[:, p].rearrange("r b n -> r (b n)"), ALU.add).then_inc(rot.sem, 1)

            def masked(g, m):
                dve.wait_ge(sc_ps.sem, sc_ps.at(g, m + 1))
                if later(g):
                    dve.wait_ge(o_ps.sem, o_ps.at(g - 1, m // 2 + 1))
                elif m == 0:
                    dve.wait_ge(mask.sem, 1)
                dve.tensor_tensor(SC[:, m].rearrange("r h n -> r (h n)"), bS[:, :],
                                  MASK[:, :, :].rearrange("r h n -> r (h n)"), ALU.mult).then_inc(sc_sb.sem, 1)

            def state(g, p):
                dve.wait_ge(kv.sem, kv.at(g, p + 1))
                if p == 1:
                    dve.wait_ge(o_ps.sem, o_ps.at(g, 1))
                elif later(g):
                    dve.wait_ge(o_ps.sem, o_ps.at(g - 1, 2))
                if p == 1:
                    dve.wait_ge(st.sem, st.at(g, 1))
                elif later(g):
                    dve.wait_ge(st.sem, st.at(g - 1, 2))
                else:
                    dve.wait_ge(s_zero.sem, 1)
                for h in range(H):
                    r, c = slice(h * DK, (h + 1) * DK), slice(h * DV, (h + 1) * DV)
                    last = dve.scalar_tensor_tensor(
                        out=S[r, 1 - p, :, c], in0=S[r, p, :, c], scalar=CN[r, GCH0:GCH0 + 1],
                        in1=bS[r, :].rearrange("r (b n) -> r b n", b=2)[:, :, c], op0=ALU.mult, op1=ALU.add)
                last.then_inc(st.sem, 1)

            def mean_squares(g, p):
                dve.wait_ge(sq.sem, sq.at(g, p + 1))
                dve.tensor_reduce(SS[:, p], SQ[:, p].rearrange("r (h v) -> r h v", v=DV), AX.X, ALU.add).then_inc(ss.sem, 1)
                dve.wait_ge(ss.sem, ss.at(g, p + 1))
                dve.tensor_scalar(MS[:, p], SS[:, p], 1.0 / DV, EPS, ALU.mult, ALU.add).then_inc(ms.sem, 1)

            def gate_out(g, p):
                dve.wait_ge(sq.sem, sq.at(g, p + 1))
                dve.wait_ge(sg.sem, sg.at(g, p + 1))
                if later(g):
                    dve.wait_ge(og.sem, og.at(g - 1, p + 1))
                dve.tensor_tensor(OGR[:, p], bO[:, :], SG[:, p].rearrange("r b n -> r (b n)"), ALU.mult).then_inc(ogr.sem, 1)

            def add_attention(g, p):
                dve.wait_ge(wo_ps.sem, wo_ps.at(g, p + 1))
                xs = cols(X, g, 2 * P, p * 2 * P)
                dve.tensor_tensor(xs, bV[:, 0:2 * P], xs, ALU.add).then_inc(x1.sem, 1)

            def stats2(g, p):
                dve.wait_ge(x1.sem, x1.at(g, p + 1))
                for m in (2 * p, 2 * p + 1):
                    last = dve.bn_stats(ST2[:, m, :], cols(X, g, P, m * P))
                last.then_inc(ln2_step.sem, 1)
                dve.wait_ge(ln2_step.sem, ln2_step.at(g, 3 * p + 1))
                for m in (2 * p, 2 * p + 1):
                    last = dve.bn_aggr(MV2[:, m, :], ST2[:, m, :])
                last.then_inc(ln2_step.sem, 1)
                dve.wait_ge(ln2_step.sem, ln2_step.at(g, 3 * p + 2))
                dve.tensor_scalar(VE2[:, 2 * p:2 * p + 2], MV2[:, 2 * p:2 * p + 2, 1], EPS, None,
                                  ALU.add).then_inc(ln2_step.sem, 1)

            def normalize2(g, p):
                dve.wait_ge(rs2.sem, rs2.at(g, p + 1))
                for m in (2 * p, 2 * p + 1):
                    last = dve.tensor_scalar(XN2[:, m * P:(m + 1) * P], cols(X, g, P, m * P), MV2[:, m, 0:1],
                                             RS2[:, m:m + 1], ALU.subtract, ALU.mult)
                last.then_inc(xn2.sem, 1)

            def x2_lo(g, p):
                dve.wait_ge(xh2.sem, xh2.at(g, p + 1))
                c = slice(p * 2 * P, (p + 1) * 2 * P)
                dve.tensor_tensor(XL2[:, c], bV[:, 0:2 * P], XH2[:, c].bitcast(F32), ALU.subtract).then_inc(xl2.sem, 1)

            def route_a(g):
                lg = bC[:, 0:TILES * E].rearrange("r (m e) -> r m e", e=E)
                dve.wait_ge(logits.sem, logits.at(g))
                dve.tensor_reduce(MX[:, :], lg, AX.X, ALU.max).then_inc(route.sem, 1)
                dve.wait_ge(route.sem, route.at(g, 1))
                dve.tensor_tensor(SHI[:, :, :], lg, MX[:, :].unsqueeze(2).to_broadcast([P, TILES, E]),
                                  ALU.subtract).then_inc(route.sem, 1)

            def route_b(g):
                wide = [P, TILES, E, E]
                step = [2]

                def then(ins):
                    step[0] += 1
                    ins.then_inc(route.sem, 1)
                    dve.wait_ge(route.sem, route.at(g, step[0]))

                dve.wait_ge(exped.sem, exped.at(g))
                then(dve.tensor_reduce(Z[:, :], EX[:, :, :], AX.X, ALU.add))
                then(dve.reciprocal(RZ[:, :], Z[:, :]))
                then(dve.tensor_tensor(PR[:, :, :], EX[:, :, :], RZ[:, :].unsqueeze(2).to_broadcast([P, TILES, E]), ALU.mult))
                then(dve.tensor_tensor(DIF[:, :, :, :], PR[:, :, :].unsqueeze(2).to_broadcast(wide),
                                       PR[:, :, :].unsqueeze(3).to_broadcast(wide), ALU.subtract))
                thr = CN[:, THR0:THR0 + E * E].unsqueeze(1).to_broadcast([P, TILES, E * E])
                then(dve.tensor_tensor(BEF[:, :, :, :].rearrange("r m i j -> r m (i j)"),
                                       DIF[:, :, :, :].rearrange("r m i j -> r m (i j)"), thr, ALU.is_ge))
                then(dve.tensor_reduce(RANK[:, :, :], BEF[:, :, :, :], AX.X, ALU.add))
                then(dve.scalar_tensor_tensor(out=WT[:, :, :], in0=RANK[:, :, :], scalar=float(TOP_K), in1=PR[:, :, :],
                                              op0=ALU.is_lt, op1=ALU.mult))
                then(dve.tensor_reduce(WS[:, :], WT[:, :, :], AX.X, ALU.add))
                then(dve.tensor_scalar(WSG[:, :], WS[:, :], 1e-20, None, ALU.add))
                then(dve.reciprocal(RWS[:, :], WSG[:, :]))
                then(dve.tensor_tensor(CMB[:, :, :], WT[:, :, :], RWS[:, :].unsqueeze(2).to_broadcast([P, TILES, E]), ALU.mult))
                if later(g):
                    dve.wait_ge(ct_ps.sem, ct_ps.at(g - 1))
                hi = CX[:, :, HI0:HI0 + E].bitcast(F32R)
                dve.tensor_copy(CX[:, :, HB0:HB0 + E].bitcast(F32R), CMB[:, :, :])
                then(dve.tensor_copy(hi, CMB[:, :, :]))
                dve.tensor_tensor(CX[:, :, LO0:LO0 + E], CMB[:, :, :], CX[:, :, HI0:HI0 + E],
                                  ALU.subtract).then_inc(comb.sem, 1)

            def gating(g, k):
                dve.wait_ge(spread.sem, spread.at(g, k))
                dve.wait_ge(hid.sem, hid.at(g, k + 1))
                if k >= 4:
                    dve.wait_ge(hg_lo.sem, hg_lo.at(g, k - 2))
                elif later(g):
                    dve.wait_ge(hg_lo.sem, hg_lo.at(g - 1, k + 4 if k == 3 else k + 7))
                dve.tensor_tensor(HG[:, k % 3, :], bC[:, :], HB[:, k % 3, :], ALU.mult).then_inc(gated.sem, 1)

            def result(g):
                dve.wait_ge(yt.sem, yt.at(g))
                if later(g):
                    dve.wait_ge(stored.sem, stored.at(g - 1, 32))
                dve.tensor_tensor(OUT[:, :, :].rearrange("r m n -> r (m n)"), bY[:, :], cols(X, g),
                                  ALU.add).then_inc(outs.sem, 1)

            def low_w():
                dve.wait_ge(w_hi.sem, 1)
                dve.tensor_tensor(WL[:, :], W[:, :], WH[:, :].bitcast(F32), ALU.subtract).then_inc(w_lo.sem, 1)

            def fold_norm():
                dve.wait_ge(ld_wo.sem, 16)
                dve.wait_ge(ld_gn.sem, 16)
                dve.tensor_scalar(WOG[:, :, :].rearrange("r a n -> r (a n)"), WO[:, :, :].rearrange("r a n -> r (a n)"),
                                  GN[:, 0:1], None, ALU.mult).then_inc(wog.sem, 1)

            def low_experts():
                dve.wait_ge(gw_hi.sem, 1)
                dve.tensor_tensor(GWL[:, :], GW[:, :], GWH[:, :].bitcast(F32), ALU.subtract).then_inc(gw_lo.sem, 1)
                dve.wait_ge(uw_hi.sem, 1)
                dve.tensor_tensor(UWL[:, :], UW[:, :], UWH[:, :].bitcast(F32), ALU.subtract).then_inc(uw_lo.sem, 1)

            def low_down():
                dve.wait_ge(dw_hi.sem, 1)
                dve.tensor_tensor(DWL[:, :], DW[:, :], DWH[:, :].bitcast(F32), ALU.subtract).then_inc(dw_lo.sem, 1)

            def low_biases():
                dve.wait_ge(db_hi.sem, 1)
                dve.tensor_tensor(DBX[HB0:P, :], DB[HB0:P, :], CT[HB0:P, 0:P].bitcast(F32),
                                  ALU.subtract).then_inc(db_lo.sem, 1)

            def selector():
                dve.wait_ge(sel_self.sem, 1)
                dve.tensor_copy(SEL[:, :, :], SELF[:, :, :]).then_inc(sel.sem, 1)

            def stats1_rest():
                for g in range(1, GROUPS):
                    dve.wait_ge(ld_x[g].sem, 32)
                stats1(TILES, GROUPS * TILES, 2)

            dve.wait_ge(ld_x[0].sem, 32)
            stats1(0, TILES, 1)
            low_w()
            normalize1(0)
            x1_lo(0)
            rotary(0, 0)
            rotate(0, 0)
            stats1_rest()
            masked(0, 0)
            masked(0, 1)
            rotary(0, 1)
            normalize1(1)
            fold_norm()
            rotate(0, 1)
            mean_squares(0, 0)
            state(0, 0)
            gate_out(0, 0)
            masked(0, 2)
            low_biases()
            masked(0, 3)
            add_attention(0, 0)
            stats2(0, 0)
            normalize2(0, 0)
            mean_squares(0, 1)
            gate_out(0, 1)
            x1_lo(1)
            x2_lo(0, 0)
            low_experts()
            selector()
            rotary(1, 0)
            add_attention(0, 1)
            stats2(0, 1)
            rotate(1, 0)
            normalize2(0, 1)
            x2_lo(0, 1)
            low_down()
            state(0, 1)

            def steady(g):
                f = g - 1
                route_a(f)
                rotary(g, 1)
                masked(g, 0)
                rotate(g, 1)
                masked(g, 1)
                route_b(f)
                mean_squares(g, 0)
                state(g, 0)
                gate_out(g, 0)
                gating(f, 1)
                masked(g, 2)
                gating(f, 2)
                if g + 1 < GROUPS:
                    normalize1(g + 1)
                masked(g, 3)
                gating(f, 3)
                add_attention(g, 0)
                stats2(g, 0)
                mean_squares(g, 1)
                gating(f, 4)
                gating(f, 5)
                if g + 1 < GROUPS:
                    x1_lo(g + 1)
                normalize2(g, 0)
                gating(f, 6)
                gate_out(g, 1)
                x2_lo(g, 0)
                gating(f, 7)
                if g + 1 < GROUPS:
                    rotary(g + 1, 0)
                gating(f, 8)
                add_attention(g, 1)
                stats2(g, 1)
                normalize2(g, 1)
                if g + 1 < GROUPS:
                    rotate(g + 1, 0)
                x2_lo(g, 1)
                result(f)
                state(g, 1)

            for g in range(1, GROUPS):
                steady(g)
            f = GROUPS - 1
            route_a(f)
            route_b(f)
            gating(f, 1)
            gating(f, 2)
            gating(f, 3)
            gating(f, 4)
            gating(f, 5)
            gating(f, 6)
            gating(f, 7)
            gating(f, 8)
            result(f)

        @block.tensor
        def _(pe):
            def keep_busy(n):
                for _ in range(n):
                    pe.matmul(bC[:, 0:P], IDN[:, :], IDN[:, :], start=True, stop=True)

            def x1_t(g):
                pe.wait_ge(xn1.sem, xn1.at(g))
                if later(g):
                    pe.wait_ge(kt.sem, kt.at(g - 1, 2))
                    pe.wait_ge(qt.sem, qt.at(g - 1, 2))
                for m in range(TILES):
                    last = pe.transpose(bX[:, m * P:(m + 1) * P], XN1[:, m * P:(m + 1) * P], IDN[:, :])
                last.then_inc(t1.sem, 1)

            def project(g, p, dst, c0, n, done):
                for b in range(2):
                    m = 2 * p + b
                    t = slice(m * P, (m + 1) * P)
                    last = product(dst[:, b * n:(b + 1) * n], (XH1[:, t], XL1[:, t]),
                                   (WH[:, c0:c0 + n], WL[:, c0:c0 + n]), True, True)
                last.then_inc(done.sem, 1)

            def proj_qk(g, p):
                if p == 0:
                    pe.wait_ge(xl1.sem, xl1.at(g))
                    if not later(g):
                        pe.wait_ge(w_lo.sem, 1)
                else:
                    pe.wait_ge(kt.sem, kt.at(g, 1))
                    pe.wait_ge(qt.sem, qt.at(g, 1))
                project(g, p, bX, 0, QK, qk)

            def proj_v(g, p):
                if p == 0:
                    pe.wait_ge(xl1.sem, xl1.at(g))
                    if later(g):
                        pe.wait_ge(xl2.sem, xl2.at(g - 1, 2))
                    else:
                        pe.wait_ge(w_lo.sem, 1)
                else:
                    pe.wait_ge(sg.sem, sg.at(g, 1))
                project(g, p, bV, QK, HV, v_ps)

            def proj_g(g, p):
                pe.wait_ge(v_sb.sem, v_sb.at(g, p + 1))
                project(g, p, bV, QK + HV, HV, g_ps)

            def qk_t(g, p):
                pe.wait_ge(rot.sem, rot.at(g, p + 1))
                for a in range(2):
                    for b in range(2):
                        o = (2 * a + b) * P
                        last = pe.transpose(bX[:, o:o + P], QKR[:, p, b, a * P:(a + 1) * P], IDN[:, :])
                last.then_inc(t2.sem, 1)

            def scores(g, m):
                p, b = divmod(m, 2)
                if b == 0:
                    pe.wait_ge(kt.sem, kt.at(g, p + 1))
                if m in (1, 3):
                    pe.wait_ge(sc_sb.sem, sc_sb.at(g, m))
                elif m == 2:
                    pe.wait_ge(st.sem, st.at(g, 1))
                elif later(g):
                    pe.wait_ge(st.sem, st.at(g - 1, 2))
                pe.matmul(bS[:, :], KT[:, p, b, :], QBD[:, p, b].rearrange("r h n -> r (h n)"), start=True,
                          stop=True).then_inc(sc_ps.sem, 1)

            def state_add(g, p):
                pe.wait_ge(sc_sb.sem, sc_sb.at(g, 2 * p + 2))
                pe.wait_ge(v_sb.sem, v_sb.at(g, p + 1))
                for b in range(2):
                    last = pe.matmul(bS[:, b * HV:(b + 1) * HV], QKR[:, p, b, P:2 * P], V[:, p, b, :],
                                     start=True, stop=True)
                last.then_inc(kv.sem, 1)

            def attend(g, p):
                pe.wait_ge(qt.sem, qt.at(g, p + 1))
                if p == 1:
                    pe.wait_ge(ogr.sem, ogr.at(g, 1))
                    pe.wait_ge(st.sem, st.at(g, 1))
                elif later(g):
                    pe.wait_ge(ogr.sem, ogr.at(g - 1, 2))
                    pe.wait_ge(st.sem, st.at(g - 1, 2))
                else:
                    pe.wait_ge(s_zero.sem, 1)
                pe.wait_ge(v_sb.sem, v_sb.at(g, p + 1))
                pe.wait_ge(sc_sb.sem, sc_sb.at(g, 2 * p + 2))
                for b in range(2):
                    pe.matmul(bO[:, b * HV:(b + 1) * HV], QT[:, p, b, :], S[:, p, b, :], start=True, stop=False)
                    for h in range(H):
                        c = slice(b * HV + h * DV, b * HV + (h + 1) * DV)
                        last = pe.matmul(bO[:, c], SC[:, 2 * p + b, h, :], V[:, p, b, h * DV:(h + 1) * DV],
                                         start=False, stop=(h == H - 1))
                last.then_inc(o_ps.sem, 1)

            def out_t(g, p):
                pe.wait_ge(og.sem, og.at(g, p + 1))
                if p == 0:
                    pe.wait_ge(sg.sem, sg.at(g, 2))
                else:
                    pe.wait_ge(xl2.sem, xl2.at(g, 1))
                for b in range(2):
                    for a in range(2):
                        o = (2 * b + a) * P
                        last = pe.transpose(bV[:, o:o + P], OG[:, p, o:o + P], IDN[:, :])
                last.then_inc(t3.sem, 1)

            def proj_out(g, p):
                pe.wait_ge(ogt.sem, ogt.at(g, p + 1))
                if not later(g):
                    pe.wait_ge(wog.sem, 1)
                for b in range(2):
                    for a in range(2):
                        last = pe.matmul(bV[:, b * P:(b + 1) * P], OGT[:, p, b, a, :], WOG[:, a, :],
                                         start=(a == 0), stop=(a == 1))
                last.then_inc(wo_ps.sem, 1)

            def x2_t(g, p):
                pe.wait_ge(xn2.sem, xn2.at(g, p + 1))
                for b in range(2):
                    m = 2 * p + b
                    last = pe.transpose(bV[:, b * P:(b + 1) * P], XN2[:, m * P:(m + 1) * P], IDN[:, :])
                last.then_inc(t4.sem, 1)

            def router(g):
                pe.wait_ge(xl2.sem, xl2.at(g, 2))
                if not later(g):
                    pe.wait_ge(gw_lo.sem, 1)
                else:
                    pe.wait_ge(gated.sem, gated.at(g - 1, E))
                for m in range(TILES):
                    t = slice(m * P, (m + 1) * P)
                    last = product(bC[:, m * E:(m + 1) * E], (XH2[:, t], XL2[:, t]), (GWH[:, :], GWL[:, :]), True, True)
                last.then_inc(logits.sem, 1)

            def comb_t(g):
                pe.wait_ge(comb.sem, comb.at(g))
                for m in range(TILES):
                    last = pe.transpose(bC[:, m * P:(m + 1) * P], CX[:, m, :], IDN[:, :])
                last.then_inc(ct_ps.sem, 1)

            def up_proj(g, k):
                e = expert(k)
                if k == 0:
                    pe.wait_ge(xl2.sem, xl2.at(g, 2))
                    if not later(g):
                        pe.wait_ge(uw_lo.sem, 1)
                if k >= 2:
                    pe.wait_ge(hid.sem, hid.at(g, k - 1))
                elif later(g):
                    pe.wait_ge(hid.sem, hid.at(g - 1, E + 1 - k))
                w = slice(e * P, (e + 1) * P)
                product(bU[k % 2][:, :], (UWH[:, w], UWL[:, w]), (XH2[:, :], XL2[:, :]), True, True).then_inc(up.sem, 1)

            def spread_comb(g, k):
                if k == 1:
                    pe.wait_ge(ct_sb.sem, ct_sb.at(g))
                    if not later(g):
                        pe.wait_ge(sel.sem, 1)
                else:
                    pe.wait_ge(gated.sem, gated.at(g, k - 1))
                pe.matmul(bC[:, :], SEL[:, expert(k), :], CT[:, :], start=True, stop=True).then_inc(spread.sem, 1)

            def down_proj(g, k):
                e = expert(k)
                pe.wait_ge(hg_lo.sem, hg_lo.at(g, k + 1))
                if k == 0:
                    if later(g):
                        pe.wait_ge(outs.sem, outs.at(g - 1))
                    else:
                        pe.wait_ge(dw_lo.sem, 1)
                if k == E:
                    pe.matmul(bY[:, :], DBX[:, :], CT[:, :], start=False, stop=False)
                w = slice(e * P, (e + 1) * P)
                product(bY[:, :], (DWH[:, w], DWL[:, w]), (HGH[:, k % 3, :], HGL[:, k % 3, :]), k == 0,
                        k == E).then_inc(down.sem, 1)

            def y_t(g):
                pe.wait_ge(y_sb.sem, y_sb.at(g))
                for m in range(TILES):
                    last = pe.transpose(bY[:, m * P:(m + 1) * P], YS[:, m * P:(m + 1) * P], IDN[:, :])
                last.then_inc(yt.sem, 1)

            pe.wait_ge(idn.sem, 1)
            keep_busy(22)
            x1_t(0)
            keep_busy(6)
            proj_qk(0, 0)
            proj_v(0, 0)
            keep_busy(1)
            qk_t(0, 0)
            keep_busy(7)
            scores(0, 0)
            keep_busy(6)
            proj_g(0, 0)
            scores(0, 1)
            proj_qk(0, 1)
            proj_v(0, 1)
            attend(0, 0)
            state_add(0, 0)
            keep_busy(1)
            qk_t(0, 1)
            proj_g(0, 1)
            keep_busy(4)
            scores(0, 2)
            keep_busy(1)
            out_t(0, 0)
            keep_busy(1)
            scores(0, 3)
            keep_busy(2)
            proj_out(0, 0)
            attend(0, 1)
            x1_t(1)
            keep_busy(3)
            x2_t(0, 0)
            state_add(0, 1)
            keep_busy(1)
            proj_qk(1, 0)
            keep_busy(2)
            out_t(0, 1)
            keep_busy(4)
            proj_out(0, 1)
            keep_busy(7)
            x2_t(0, 1)

            def steady(g):
                f = g - 1
                qk_t(g, 0)
                router(f)
                proj_v(g, 0)
                proj_qk(g, 1)
                scores(g, 0)
                up_proj(f, 0)
                proj_g(g, 0)
                up_proj(f, 1)
                scores(g, 1)
                up_proj(f, 2)
                qk_t(g, 1)
                attend(g, 0)
                state_add(g, 0)
                comb_t(f)
                proj_v(g, 1)
                up_proj(f, 3)
                spread_comb(f, 1)
                proj_g(g, 1)
                scores(g, 2)
                spread_comb(f, 2)
                down_proj(f, 0)
                out_t(g, 0)
                scores(g, 3)
                spread_comb(f, 3)
                proj_out(g, 0)
                attend(g, 1)
                up_proj(f, 4)
                down_proj(f, 1)
                spread_comb(f, 4)
                if g + 1 < GROUPS:
                    x1_t(g + 1)
                up_proj(f, 5)
                up_proj(f, 6)
                spread_comb(f, 5)
                down_proj(f, 2)
                up_proj(f, 7)
                spread_comb(f, 6)
                up_proj(f, 8)
                x2_t(g, 0)
                down_proj(f, 3)
                spread_comb(f, 7)
                if g + 1 < GROUPS:
                    proj_qk(g + 1, 0)
                down_proj(f, 4)
                spread_comb(f, 8)
                out_t(g, 1)
                down_proj(f, 5)
                proj_out(g, 1)
                down_proj(f, 6)
                down_proj(f, 7)
                down_proj(f, 8)
                state_add(g, 1)
                x2_t(g, 1)
                y_t(f)

            for g in range(1, GROUPS):
                steady(g)
            f = GROUPS - 1
            router(f)
            up_proj(f, 0)
            up_proj(f, 1)
            up_proj(f, 2)
            up_proj(f, 3)
            comb_t(f)
            spread_comb(f, 1)
            down_proj(f, 0)
            spread_comb(f, 2)
            up_proj(f, 4)
            spread_comb(f, 3)
            up_proj(f, 5)
            spread_comb(f, 4)
            up_proj(f, 6)
            spread_comb(f, 5)
            down_proj(f, 1)
            up_proj(f, 7)
            spread_comb(f, 6)
            down_proj(f, 2)
            up_proj(f, 8)
            down_proj(f, 3)
            spread_comb(f, 7)
            down_proj(f, 4)
            spread_comb(f, 8)
            down_proj(f, 5)
            down_proj(f, 6)
            down_proj(f, 7)
            down_proj(f, 8)
            y_t(f)



def kernel(**inputs):
    import concourse.bacc as bacc
    from concourse.bass_utils import run_bass_kernel_spmd

    def arr(name):
        return np.asarray(inputs[name])

    both = np.concatenate
    feeds = {
        "x": arr("L0_attn_x"),
        "wqkvg": both([arr("L0_attn_" + n) for n in ("Wq", "Wk", "Wv", "Wg")], axis=0).T,
        "wot": arr("L0_attn_Wo").T.reshape(2, P, P).transpose(1, 0, 2),
        "gnw": np.tile(arr("L0_attn_g_norm_w"), P // DV)[:, None],
        "upw": both([arr("L0_ffn_up_w"), arr("L0_ffn_sh_up_w")[None]]).transpose(1, 0, 2).reshape(P, -1),
        "upb": both([arr("L0_ffn_up_b"), arr("L0_ffn_sh_up_b")[None]]).T,
        "dnw": both([arr("L0_ffn_down_w"), arr("L0_ffn_sh_down_w")[None]]).transpose(1, 0, 2).reshape(P, -1),
        "dnb": both([arr("L0_ffn_down_b"), arr("L0_ffn_sh_down_b")[None]]),
        "gatew": arr("L0_ffn_gate_w").T,
        "const": constants(),
    }
    feeds = {name: np.ascontiguousarray(a) for name, a in feeds.items()}
    nc = bacc.Bacc("TRN2", target_bir_lowering=False, num_devices=1)
    args = [nc.dram_tensor(name, a.shape, mybir.dt.from_np(a.dtype), kind="ExternalInput").ap()
            for name, a in feeds.items()]
    args.append(nc.dram_tensor("out", (B, T, P), F32, kind="ExternalOutput").ap())
    retention_moe_kernel(nc, *args)
    done = run_bass_kernel_spmd(nc, [feeds], core_ids=[0])
    return done.results[0]["out"]
```

```python
from contextlib import ExitStack

import numpy as np

import concourse.bass as bass
from concourse import mybir

F32 = mybir.dt.float32
F32R = mybir.dt.float32r
ALU = mybir.AluOpType
ACT = mybir.ActivationFunctionType
AX = mybir.AxisListType

P = 128
B = 2
T = 1024
H = 4
DK = 32
DV = 64
HV = H * DV
QK = 2 * H * DK
E = 8
TOP_K = 2
EPS = 1e-5
ROPE_BASE = 10000.0
CHUNKS = T // P
GROUPS = CHUNKS // 2
TILES = 4
GC = TILES * P
GAMMA = [1.0 - 2.0 ** (-5 - h) for h in range(H)]

ROT0 = 0
ROTW = 3 * (DK // 2)
DEC0 = ROT0 + CHUNKS * ROTW
THR0 = DEC0 + 2 * H
GCH0 = THR0 + E * E
NCONST = GCH0 + 1

HI0, LO0, HB0 = 0, 32, 64


def constants():
    half = DK // 2
    inv = (1.0 / np.float32(ROPE_BASE) ** (np.arange(0, DK, 2, dtype=np.float32) / np.float32(DK))).astype(np.float32)
    angle = (np.arange(T, dtype=np.float32)[:, None] * inv[None, :]).astype(np.float64)
    cos, sin = np.cos(angle), np.sin(angle)
    rot = np.concatenate([cos, -sin, sin], axis=1).reshape(CHUNKS, P, ROTW).transpose(1, 0, 2)
    token = np.arange(P, dtype=np.float64)[:, None]
    gamma = np.array(GAMMA)[None, :]
    dec_q = gamma ** (token + 1.0) * DK ** -0.5
    dec_k = gamma ** (P - 1.0 - token)
    i, j = np.arange(E)[:, None], np.arange(E)[None, :]
    thr = np.where(j < i, 0.0, np.where(j > i, float(np.finfo(np.float32).tiny), 1e30))
    gch = np.repeat(np.array(GAMMA) ** P, DK)[:, None]
    return np.concatenate([rot.reshape(P, -1), dec_q, dec_k, np.tile(thr.reshape(1, -1), (P, 1)), gch],
                          axis=1).astype(np.float32)


def later(g):
    return not (isinstance(g, int) and g == 0)


class Signal:

    def __init__(self, sem, per, primed):
        self.sem, self.per, self.primed = sem, per, primed

    def at(self, g, n=1):
        return (g + 1 if self.primed else g) * self.per + n


def retention_moe_kernel(nc, x, wqkvg, wot, gnw, upw, upb, dnw, dnb, gatew, const, out):
    ctx = ExitStack()
    with ctx:
        def sb(name, shape, dt=F32):
            return ctx.enter_context(nc.sbuf_tensor(name, shape, dt))

        def bank(name):
            return ctx.enter_context(nc.psum_tensor(name, [P, 512], F32))

        def sig(name, per=1, primed=False):
            return Signal(ctx.enter_context(nc.semaphore(name)), per, primed)

        X = sb("X", [P, GROUPS * GC])
        W = sb("W", [P, QK + 2 * HV])
        WH = sb("WH", [P, QK + 2 * HV], F32R)
        WL = sb("WL", [P, QK + 2 * HV], F32R)
        WO = sb("WO", [P, 2, P])
        WOG = sb("WOG", [P, 2, P])
        GN = sb("GN", [P, 1])
        UW = sb("UW", [P, (E + 1) * P])
        UWH = sb("UWH", [P, (E + 1) * P], F32R)
        UWL = sb("UWL", [P, (E + 1) * P], F32R)
        UB = sb("UB", [P, E + 1])
        DW = sb("DW", [P, (E + 1) * P])
        DWH = sb("DWH", [P, (E + 1) * P], F32R)
        DWL = sb("DWL", [P, (E + 1) * P], F32R)
        DB = sb("DB", [P, P])
        DBX = sb("DBX", [P, P], F32R)
        GW = sb("GW", [P, E])
        GWS = sb("GWS", [P, 2, E], F32R)
        CN = sb("CN", [P, NCONST])
        COS = sb("COS", [P, CHUNKS * QK])
        SIN = sb("SIN", [P, CHUNKS * QK])
        IDN = sb("IDN", [P, P])
        MASK = sb("MASK", [P, H, P])
        SELF = sb("SELF", [P, E, P])
        SEL = sb("SEL", [P, E, P], F32R)
        NHALF = sb("NHALF", [P, 2 * H])
        WARM = sb("WARM", [P, 1])

        ST1 = sb("ST1", [P, TILES, 6])
        MV1 = sb("MV1", [P, GROUPS * TILES * 2])
        VE1 = sb("VE1", [P, GROUPS * TILES])
        RS1 = sb("RS1", [P, GROUPS * TILES])
        XN1 = sb("XN1", [P, GC])
        XH1 = sb("XH1", [P, GC], F32R)
        XL1 = sb("XL1", [P, GC], F32R)
        RA = sb("RA", [P, 2, 2, QK])
        RB = sb("RB", [P, 2, 2, QK])
        QKR = sb("QKR", [P, 2, 2, QK])
        V = sb("V", [P, 2, 2, HV])
        SG = sb("SG", [P, 2, 2, HV])
        QT = sb("QT", [P, 2, 2, P])
        KT = sb("KT", [P, 2, 2, P])
        QBD = sb("QBD", [P, 2, 2, H, P])
        SC = sb("SC", [P, TILES, H, P])
        S = sb("S", [P, 2, 2, HV])
        SQ = sb("SQ", [P, 2, 2 * HV])
        SS = sb("SS", [P, 2, 2 * H])
        MS = sb("MS", [P, 2, 2 * H])
        RR = sb("RR", [P, 2, 2 * H])
        OGR = sb("OGR", [P, 2, 2 * HV])
        OG = sb("OG", [P, 2, 2 * HV])
        OGT = sb("OGT", [P, 2, 2, 2, P])
        X1 = sb("X1", [P, GC])
        ST2 = sb("ST2", [P, TILES, 6])
        MV2 = sb("MV2", [P, TILES, 2])
        VE2 = sb("VE2", [P, TILES])
        RS2 = sb("RS2", [P, TILES])
        XN2 = sb("XN2", [P, GC])
        XH2 = sb("XH2", [P, GC], F32R)
        XL2 = sb("XL2", [P, GC], F32R)

        LG = sb("LG", [P, TILES, E])
        MX = sb("MX", [P, TILES])
        SHI = sb("SHI", [P, TILES, E])
        EX = sb("EX", [P, TILES, E])
        Z = sb("Z", [P, TILES])
        RZ = sb("RZ", [P, TILES])
        PR = sb("PR", [P, TILES, E])
        DIF = sb("DIF", [P, TILES, E, E])
        BEF = sb("BEF", [P, TILES, E, E])
        RANK = sb("RANK", [P, TILES, E])
        WT = sb("WT", [P, TILES, E])
        WS = sb("WS", [P, TILES])
        WSG = sb("WSG", [P, TILES])
        RWS = sb("RWS", [P, TILES])
        CMB = sb("CMB", [P, TILES, E])
        CX = sb("CX", [P, TILES, P])
        CT = sb("CT", [P, GC], F32R)
        HB = sb("HB", [P, E + 1, GC])
        HG = sb("HG", [P, 3, GC])
        HGH = sb("HGH", [P, 3, GC], F32R)
        HGL = sb("HGL", [P, 3, GC], F32R)
        YS = sb("YS", [P, GC])
        OUT = sb("OUT", [P, TILES, P])

        bX = bank("bX")
        bV = bank("bV")
        bS = bank("bS")
        bO = bank("bO")
        bU = [bank("bU0"), bank("bU1")]
        bC = bank("bC")
        bY = bank("bY")

        ld_x = [sig(f"ld_x{g}") for g in range(GROUPS)]
        ld_w, ld_c, ld_wo, ld_gn, ld_up, ld_ub, ld_dn, ld_db, ld_gw = (
            sig(n) for n in ("ld_w", "ld_c", "ld_wo", "ld_gn", "ld_up", "ld_ub", "ld_dn", "ld_db", "ld_gw"))
        db_zero, idn_zero, idn, mask_fill, mask, sel_zero, sel_first, sel_self, sel, nhalf, tables, s_zero, bd_zero, cx_set = (
            sig(n) for n in ("db_zero", "idn_zero", "idn", "mask_fill", "mask", "sel_zero", "sel_first", "sel_self",
                             "sel", "nhalf", "tables", "s_zero", "bd_zero", "cx_set"))
        w_hi, w_lo, uw_hi, uw_lo, dw_hi, dw_lo, gw_hi, gw_lo, wog, db_hi, db_lo = (
            sig(n) for n in ("w_hi", "w_lo", "uw_hi", "uw_lo", "dw_hi", "dw_lo", "gw_hi", "gw_lo", "wog", "db_hi", "db_lo"))
        ln1_stats, ln1_step, rs1 = sig("ln1_stats", 2), sig("ln1_step"), sig("rs1")
        xn1, t1, xh1, xl1 = sig("xn1"), sig("t1"), sig("xh1"), sig("xl1")
        qk, v_ps, g_ps, rparts, rot, v_sb, sg = (sig(n, 2) for n in ("qk", "v_ps", "g_ps", "rparts", "rot", "v_sb", "sg"))
        t2, kt, qt = sig("t2", 2), sig("kt", 2), sig("qt", 2)
        sc_ps, sc_sb = sig("sc_ps", TILES), sig("sc_sb", TILES)
        kv, st, o_ps, sq, ss, ms, rr, ogr, og = (
            sig(n, 2) for n in ("kv", "st", "o_ps", "sq", "ss", "ms", "rr", "ogr", "og"))
        t3, ogt, wo_ps, x1, kept = (sig(n, 2) for n in ("t3", "ogt", "wo_ps", "x1", "kept"))
        ln2_step = sig("ln2_step", 6)
        rs2, xn2, t4, xh2, xl2 = (sig(n, 2) for n in ("rs2", "xn2", "t4", "xh2", "xl2"))
        logits, exped, comb, ct_sb = (sig(n) for n in ("logits", "exped", "comb", "ct_sb"))
        ct_ps = sig("ct_ps", primed=True)
        route = sig("route", 15)
        up, hid, down = sig("up", E + 1), sig("hid", E + 1, primed=True), sig("down", E + 1, primed=True)
        spread, gated = sig("spread", E), sig("gated", E, primed=True)
        hg_hi, hg_lo = sig("hg_hi", E + 1), sig("hg_lo", E + 1, primed=True)
        y_sb, yt, outs = sig("y_sb"), sig("yt", primed=True), sig("outs", primed=True)
        stored = sig("stored", 32, primed=True)

        def first(g):
            return isinstance(g, int) and g == 0

        def qk_bank(g, p):
            return bU[0] if first(g) and p == 1 else bX

        def v_bank(g, p):
            return bU[1] if first(g) and p == 1 else bV

        def score_bank(g, m):
            return bC if first(g) and m in (1, 2) else bS

        def tail_bank(g, p):
            return bU[1] if first(g) and p == 1 else bV

        block = ctx.enter_context(nc.Block())

        def product(out_, wide, narrow, start, stop):
            (ah, al), (bh, bl) = wide, narrow
            nc.tensor.matmul(out_, ah, bh, start=start, stop=False)
            nc.tensor.matmul(out_, ah, bl, start=False, stop=False)
            return nc.tensor.matmul(out_, al, bh, start=False, stop=stop)

        def expert(k):
            return E if k == 0 else k - 1

        def cols(t, g, n=GC, off=0):
            return t[:, bass.ds(g * GC + off, n)]

        def load_x(eng, g, b):
            dst = X[:, g * GC:(g + 1) * GC].rearrange("r (c b d) -> r b c d", c=2, b=B)[:, b]
            src = x[b, 2 * g * P:(2 * g + 2) * P, :].rearrange("(c r) d -> r c d", r=P)
            eng.dma_start(dst, src).then_inc(ld_x[g].sem, 16)

        @block.sync
        def _(sp):
            load_x(sp, 0, 0)
            sp.dma_start(CN[:, :], const).then_inc(ld_c.sem, 16)
            sp.dma_start(GW[:, :], gatew).then_inc(ld_gw.sem, 16)
            sp.dma_start(UW[:, :], upw).then_inc(ld_up.sem, 16)
            for g in range(1, GROUPS):
                for b in range(B):
                    load_x(sp, g, b)
            sp.dma_start(DW[:, :], dnw).then_inc(ld_dn.sem, 16)
            sp.dma_start(WO[:, :, :], wot).then_inc(ld_wo.sem, 16)
            sp.dma_start(GN[:, :], gnw).then_inc(ld_gn.sem, 16)
            sp.dma_start(UB[:, :], upb).then_inc(ld_ub.sem, 16)
            sp.wait_ge(db_zero.sem, 1)
            for r0, n in ((HI0, E + 1), (LO0, E), (HB0, E + 1)):
                sp.dma_start(DB[r0:r0 + n, :], dnb[0:n, :]).then_inc(ld_db.sem, 16)

            def store(g):
                sp.wait_ge(outs.sem, outs.at(g))
                for b in range(B):
                    dst = out[b].rearrange("(g c r) d -> g r c d", c=2, r=P)[g]
                    src = OUT[:, :, :].rearrange("r (c b) d -> r b c d", b=B)[:, b]
                    sp.dma_start(dst, src).then_inc(stored.sem, 16)

            for g in range(GROUPS):
                store(g)
            sp.wait_ge(stored.sem, stored.at(GROUPS - 1, 32))

        @block.gpsimd
        def _(pool):
            pool.memset(NHALF[:, :], -0.5).then_inc(nhalf.sem, 1)
            pool.memset(IDN[:, :], 0.0).then_inc(idn_zero.sem, 1)
            pool.wait_ge(idn_zero.sem, 1)
            pool.affine_select(out=IDN[:, :], in_=IDN[:, :], compare_op=ALU.not_equal, fill=1.0, base=0,
                               pattern=[[-1, P]], channel_multiplier=1).then_inc(idn.sem, 1)
            pool.memset(QBD[:, 0, 0], 0.0).then_inc(hg_lo.sem, hg_lo.per)
            pool.memset(QBD[:, 0, 1], 0.0).then_inc(down.sem, down.per)
            pool.memset(QBD[:, 1, 0], 0.0).then_inc(gated.sem, gated.per)
            pool.memset(QBD[:, 1, 1], 0.0).then_inc(bd_zero.sem, 1)
            pool.memset(S[:, 0], 0.0).then_inc(hid.sem, hid.per)
            pool.memset(S[:, 1], 0.0).then_inc(s_zero.sem, 1)

            def rstd1(g):
                if not later(g):
                    pool.wait_ge(nhalf.sem, 1)
                pool.wait_ge(ln1_step.sem, ln1_step.at(g))
                pool.tensor_tensor(RS1[:, bass.ds(g * TILES, TILES)], VE1[:, bass.ds(g * TILES, TILES)],
                                   NHALF[:, 0:TILES], ALU.pow).then_inc(rs1.sem, 1)

            def tables_of(*chunks):
                pool.wait_ge(ld_c.sem, 16)
                for c in chunks:
                    table(c)

            def table(c):
                dec = CN[:, DEC0:DEC0 + 2 * H]
                r0 = ROT0 + c * ROTW
                half = DK // 2
                cos = CN[:, r0:r0 + half]
                sin = CN[:, r0 + half:r0 + ROTW]
                pool.tensor_tensor(
                    COS[:, c * QK:(c + 1) * QK].rearrange("r (h a f) -> r h a f", a=2, f=half),
                    cos.unsqueeze(1).unsqueeze(1).to_broadcast([P, 2 * H, 2, half]),
                    dec.unsqueeze(2).unsqueeze(2).to_broadcast([P, 2 * H, 2, half]), ALU.mult)
                pool.tensor_tensor(
                    SIN[:, c * QK:(c + 1) * QK].rearrange("r (h f) -> r h f", f=DK),
                    sin.unsqueeze(1).to_broadcast([P, 2 * H, DK]),
                    dec.unsqueeze(2).to_broadcast([P, 2 * H, DK]), ALU.mult).then_inc(tables.sem, 1)

            def causal_mask():
                fills = [pool.memset(MASK[:, h, :], GAMMA[h] ** -P) for h in range(H)]
                fills[0].then_inc(outs.sem, outs.per)
                fills[1].then_inc(stored.sem, stored.per)
                fills[2].then_inc(ct_ps.sem, ct_ps.per)
                fills[3].then_inc(mask_fill.sem, 1)
                pool.wait_ge(mask_fill.sem, 1)
                pool.affine_select(out=MASK[:, :, :], in_=MASK[:, :, :], compare_op=ALU.is_ge, fill=0.0, base=0,
                                   pattern=[[0, H], [1, P]], channel_multiplier=-1).then_inc(mask.sem, 1)

            def rms(g, p):
                pool.wait_ge(ms.sem, ms.at(g, p + 1))
                pool.tensor_tensor(RR[:, p], MS[:, p], NHALF[:, 0:2 * H], ALU.pow).then_inc(rr.sem, 1)

            def normalize_out(g, p):
                pool.wait_ge(rr.sem, rr.at(g, p + 1))
                pool.wait_ge(ogr.sem, ogr.at(g, p + 1))
                if later(g):
                    pool.wait_ge(t3.sem, t3.at(g - 1, p + 1))
                pool.tensor_tensor(OG[:, p].rearrange("r (h v) -> r h v", v=DV),
                                   OGR[:, p].rearrange("r (h v) -> r h v", v=DV),
                                   RR[:, p].unsqueeze(2).to_broadcast([P, 2 * H, DV]), ALU.mult).then_inc(og.sem, 1)

            def gated_lo(g, k):
                pool.wait_ge(hg_hi.sem, hg_hi.at(g, k + 1))
                pool.tensor_tensor(HGL[:, k % 3, :], HB[:, 0, :] if k == 0 else HG[:, k % 3, :],
                                   HGH[:, k % 3, :].bitcast(F32), ALU.subtract).then_inc(hg_lo.sem, 1)

            def keep_x1(g, p):
                pool.wait_ge(x1.sem, x1.at(g, p + 1))
                pool.tensor_copy(cols(X, g, 2 * P, p * 2 * P), X1[:, p * 2 * P:(p + 1) * 2 * P]).then_inc(kept.sem, 1)

            def rstd2(g, p):
                pool.wait_ge(ln2_step.sem, ln2_step.at(g, 3 * p + 3))
                pool.tensor_tensor(RS2[:, 2 * p:2 * p + 2], VE2[:, 2 * p:2 * p + 2], NHALF[:, 0:2],
                                   ALU.pow).then_inc(rs2.sem, 1)

            def selector():
                pool.memset(SELF[:, :, :], 0.0).then_inc(sel_zero.sem, 1)
                pool.wait_ge(sel_zero.sem, 1)
                pool.affine_select(out=SELF[:, :, :], in_=SELF[:, :, :], compare_op=ALU.not_equal, fill=1.0, base=-HI0,
                                   pattern=[[-1, E], [0, P]], channel_multiplier=1).then_inc(sel_first.sem, 1)
                pool.wait_ge(sel_first.sem, 1)
                pool.affine_select(out=SELF[:, :, :], in_=SELF[:, :, :], compare_op=ALU.not_equal, fill=1.0, base=-LO0,
                                   pattern=[[-1, E], [0, P]], channel_multiplier=1).then_inc(sel_self.sem, 1)

            rstd1(0)
            tables_of(0)
            causal_mask()
            tables_of(1)
            tables_of(*range(2, CHUNKS))
            rstd1(1)
            rms(0, 0)
            normalize_out(0, 0)
            selector()
            rstd2(0, 0)
            rms(0, 1)
            normalize_out(0, 1)
            rstd2(0, 1)
            keep_x1(0, 0)
            keep_x1(0, 1)

            def steady(g):
                f = g - 1
                rstd1(g + 1)
                rms(g, 0)
                gated_lo(f, 0)
                normalize_out(g, 0)
                rms(g, 1)
                normalize_out(g, 1)
                rstd2(g, 0)
                keep_x1(g, 0)
                gated_lo(f, 1)
                gated_lo(f, 2)
                gated_lo(f, 3)
                gated_lo(f, 4)
                rstd2(g, 1)
                gated_lo(f, 5)
                gated_lo(f, 6)
                gated_lo(f, 7)
                gated_lo(f, 8)
                keep_x1(g, 1)

            with pool.Fori(1, GROUPS - 1) as g:
                steady(g)
            g, f = GROUPS - 1, GROUPS - 2
            rms(g, 0)
            normalize_out(g, 0)
            rms(g, 1)
            normalize_out(g, 1)
            rstd2(g, 0)
            gated_lo(f, 0)
            gated_lo(f, 1)
            gated_lo(f, 2)
            gated_lo(f, 3)
            gated_lo(f, 4)
            rstd2(g, 1)
            gated_lo(f, 5)
            gated_lo(f, 6)
            gated_lo(f, 7)
            keep_x1(g, 0)
            gated_lo(f, 8)
            gated_lo(g, 0)
            gated_lo(g, 1)
            gated_lo(g, 2)
            gated_lo(g, 3)
            gated_lo(g, 4)
            gated_lo(g, 5)
            gated_lo(g, 6)
            gated_lo(g, 7)
            gated_lo(g, 8)
            keep_x1(g, 1)

        @block.scalar
        def _(act):
            load_x(act, 0, 1)
            act.dma_start(W[:, :], wqkvg).then_inc(ld_w.sem, 16)
            act.wait_ge(nhalf.sem, 1)
            act.activation(WARM[:, :], NHALF[:, 0:1], ACT.Silu)

            def x1_hi(g):
                act.wait_ge(t1.sem, t1.at(g))
                if later(g):
                    act.wait_ge(qk.sem, qk.at(g - 1, 2))
                    act.wait_ge(g_ps.sem, g_ps.at(g - 1, 2))
                act.copy(XH1[:, :], bX[:, :]).then_inc(xh1.sem, 1)

            def values(g, p):
                act.wait_ge(v_ps.sem, v_ps.at(g, p + 1))
                if later(g):
                    act.wait_ge(kv.sem, kv.at(g - 1, p + 1))
                    act.wait_ge(o_ps.sem, o_ps.at(g - 1, p + 1))
                act.copy(V[:, p].rearrange("r b n -> r (b n)"), v_bank(g, p)[:, :]).then_inc(v_sb.sem, 1)

            def gates(g, p):
                act.wait_ge(g_ps.sem, g_ps.at(g, p + 1))
                if later(g):
                    act.wait_ge(ogr.sem, ogr.at(g - 1, p + 1))
                act.activation(SG[:, p].rearrange("r b n -> r (b n)"), bV[:, :], ACT.Silu).then_inc(sg.sem, 1)

            def keys_t(g, p):
                act.wait_ge(t2.sem, t2.at(g, p + 1))
                if later(g):
                    act.wait_ge(o_ps.sem, o_ps.at(g - 1, p + 1))
                elif p == 0:
                    act.wait_ge(bd_zero.sem, 1)
                act.copy(KT[:, p].rearrange("r b n -> r (b n)"), bX[:, 2 * P:4 * P])
                for h in range(H):
                    r = slice(h * DK, (h + 1) * DK)
                    last = act.copy(QBD[r, p, :, h, :], bX[r, 0:2 * P].rearrange("r (b n) -> r b n", b=2))
                last.then_inc(kt.sem, 1)

            def queries_t(g, p):
                act.wait_ge(t2.sem, t2.at(g, p + 1))
                if later(g):
                    act.wait_ge(o_ps.sem, o_ps.at(g - 1, p + 1))
                act.copy(QT[:, p].rearrange("r b n -> r (b n)"), bX[:, 0:2 * P]).then_inc(qt.sem, 1)

            def squares(g, p):
                act.wait_ge(o_ps.sem, o_ps.at(g, p + 1))
                if later(g):
                    act.wait_ge(ss.sem, ss.at(g - 1, p + 1))
                act.activation(SQ[:, p], bO[:, :], ACT.Square).then_inc(sq.sem, 1)

            def transposed_out(g, p):
                act.wait_ge(t3.sem, t3.at(g, p + 1))
                if later(g):
                    act.wait_ge(wo_ps.sem, wo_ps.at(g - 1, p + 1))
                act.copy(OGT[:, p].rearrange("r b a n -> r (b a n)"), tail_bank(g, p)[:, :]).then_inc(ogt.sem, 1)

            def x2_hi(g, p):
                act.wait_ge(t4.sem, t4.at(g, p + 1))
                if later(g):
                    act.wait_ge(up.sem, up.at(g - 1, E + 1))
                act.copy(XH2[:, p * 2 * P:(p + 1) * 2 * P], tail_bank(g, p)[:, 0:2 * P]).then_inc(xh2.sem, 1)

            def hidden(g, k):
                e = expert(k)
                act.wait_ge(up.sem, up.at(g, k + 1))
                if later(g) and k == 0:
                    act.wait_ge(hg_lo.sem, hg_lo.at(g - 1, 1))
                elif later(g):
                    act.wait_ge(gated.sem, gated.at(g - 1, k))
                act.activation(HB[:, k, :], bU[k % 2][:, :], ACT.Silu, bias=UB[:, e:e + 1]).then_inc(hid.sem, 1)

            def gated_hi(g, k):
                if k == 0:
                    act.wait_ge(hid.sem, hid.at(g, 1))
                else:
                    act.wait_ge(gated.sem, gated.at(g, k))
                if k >= 3:
                    act.wait_ge(down.sem, down.at(g, k - 2))
                elif later(g):
                    act.wait_ge(down.sem, down.at(g - 1, k + 7))
                act.copy(HGH[:, k % 3, :], HB[:, 0, :] if k == 0 else HG[:, k % 3, :]).then_inc(hg_hi.sem, 1)

            def exps(g):
                act.wait_ge(route.sem, route.at(g, 3))
                act.activation(EX[:, :, :], SHI[:, :, :], ACT.Exp).then_inc(exped.sem, 1)

            def comb_sb(g):
                act.wait_ge(ct_ps.sem, ct_ps.at(g))
                if later(g):
                    act.wait_ge(down.sem, down.at(g - 1, E + 1))
                act.copy(CT[:, :], bC[:, :]).then_inc(ct_sb.sem, 1)

            def sums(g):
                act.wait_ge(down.sem, down.at(g, E + 1))
                if later(g):
                    act.wait_ge(yt.sem, yt.at(g - 1))
                act.copy(YS[:, :], bY[:, :]).then_inc(y_sb.sem, 1)

            def split_w():
                act.wait_ge(ld_w.sem, 16)
                act.copy(WH[:, :], W[:, :]).then_inc(w_hi.sem, 1)

            def split_experts():
                act.wait_ge(ld_gw.sem, 16)
                act.copy(GWS[:, 0, :], GW[:, :]).then_inc(gw_hi.sem, 1)
                act.wait_ge(ld_up.sem, 16)
                act.copy(UWH[:, :], UW[:, :]).then_inc(uw_hi.sem, 1)
                act.wait_ge(ld_db.sem, 48)
                act.copy(DBX[0:HB0, :], DB[0:HB0, :])
                act.copy(CT[HB0:P, 0:P], DB[HB0:P, :]).then_inc(db_hi.sem, 1)

            def split_down():
                act.wait_ge(ld_dn.sem, 16)
                act.copy(DWH[:, :], DW[:, :]).then_inc(dw_hi.sem, 1)

            split_w()
            x1_hi(0)
            split_experts()
            values(0, 0)
            keys_t(0, 0)
            values(0, 1)
            queries_t(0, 0)
            gates(0, 0)
            split_down()
            keys_t(0, 1)
            queries_t(0, 1)
            squares(0, 0)
            x1_hi(1)
            gates(0, 1)
            transposed_out(0, 0)
            squares(0, 1)
            keys_t(1, 0)
            x2_hi(0, 0)
            queries_t(1, 0)
            transposed_out(0, 1)
            values(1, 0)
            gates(1, 0)
            squares(1, 0)
            x2_hi(0, 1)
            act.wait_ge(ld_ub.sem, 16)
            act.wait_ge(db_lo.sem, 1)

            def steady(g):
                f = g - 1
                keys_t(g, 1)
                values(g, 1)
                queries_t(g, 1)
                hidden(f, 0)
                gated_hi(f, 0)
                exps(f)
                gates(g, 1)
                hidden(f, 1)
                hidden(f, 2)
                x1_hi(g + 1)
                squares(g, 1)
                hidden(f, 3)
                transposed_out(g, 0)
                hidden(f, 4)
                comb_sb(f)
                hidden(f, 5)
                hidden(f, 6)
                gated_hi(f, 1)
                gated_hi(f, 2)
                x2_hi(g, 0)
                gated_hi(f, 3)
                transposed_out(g, 1)
                gated_hi(f, 4)
                keys_t(g + 1, 0)
                hidden(f, 7)
                queries_t(g + 1, 0)
                gated_hi(f, 5)
                gated_hi(f, 6)
                x2_hi(g, 1)
                gated_hi(f, 7)
                values(g + 1, 0)
                hidden(f, 8)
                gated_hi(f, 8)
                squares(g + 1, 0)
                gates(g + 1, 0)
                sums(f)

            with act.Fori(1, GROUPS - 1) as g:
                steady(g)
            g, f = GROUPS - 1, GROUPS - 2
            keys_t(g, 1)
            hidden(f, 0)
            queries_t(g, 1)
            exps(f)
            values(g, 1)
            hidden(f, 1)
            gates(g, 1)
            hidden(f, 2)
            gated_hi(f, 0)
            squares(g, 1)
            transposed_out(g, 0)
            comb_sb(f)
            hidden(f, 3)
            hidden(f, 4)
            hidden(f, 5)
            gated_hi(f, 1)
            hidden(f, 6)
            hidden(f, 7)
            gated_hi(f, 2)
            x2_hi(g, 0)
            gated_hi(f, 3)
            transposed_out(g, 1)
            gated_hi(f, 4)
            hidden(f, 8)
            gated_hi(f, 5)
            gated_hi(f, 6)
            x2_hi(g, 1)
            gated_hi(f, 7)
            gated_hi(f, 8)
            hidden(g, 0)
            exps(g)
            hidden(g, 1)
            hidden(g, 2)
            sums(f)
            hidden(g, 3)
            gated_hi(g, 0)
            comb_sb(g)
            hidden(g, 4)
            hidden(g, 5)
            gated_hi(g, 1)
            gated_hi(g, 2)
            hidden(g, 6)
            gated_hi(g, 3)
            gated_hi(g, 4)
            gated_hi(g, 5)
            hidden(g, 7)
            gated_hi(g, 6)
            hidden(g, 8)
            gated_hi(g, 7)
            gated_hi(g, 8)
            sums(g)

        @block.vector
        def _(dve):
            dve.memset(DB[:, :], 0.0).then_inc(db_zero.sem, 1)
            dve.memset(CX[:, :, :], 0.0).then_inc(cx_set.sem, 1)
            dve.wait_ge(cx_set.sem, 1)
            dve.memset(CX[:, :, HI0 + E:HI0 + E + 1], 1.0).then_inc(yt.sem, yt.per)
            dve.memset(CX[:, :, HB0 + E:HB0 + E + 1], 1.0).then_inc(cx_set.sem, 1)

            def stats1(g):
                dve.wait_ge(ld_x[g].sem, 32)
                if later(g):
                    dve.wait_ge(ln1_stats.sem, ln1_stats.at(g - 1, 2))
                for m in range(TILES):
                    t = g * TILES + m
                    last = dve.bn_stats(ST1[:, m, :], X[:, t * P:(t + 1) * P])
                last.then_inc(ln1_stats.sem, 1)
                dve.wait_ge(ln1_stats.sem, ln1_stats.at(g, 1))
                for m in range(TILES):
                    t = g * TILES + m
                    last = dve.bn_aggr(MV1[:, 2 * t:2 * t + 2], ST1[:, m, :])
                last.then_inc(ln1_stats.sem, 1)
                dve.wait_ge(ln1_stats.sem, ln1_stats.at(g, 2))
                t = slice(g * TILES, (g + 1) * TILES)
                var = MV1[:, :].rearrange("r (t s) -> r t s", s=2)[:, t, 1]
                dve.tensor_scalar(VE1[:, t], var, EPS, None, ALU.add).then_inc(ln1_step.sem, 1)

            def normalize1(g):
                dve.wait_ge(rs1.sem, rs1.at(g))
                if later(g):
                    dve.wait_ge(t1.sem, t1.at(g - 1))
                for m in range(TILES):
                    mean = MV1[:, bass.ds(g * 2 * TILES + 2 * m, 1)]
                    rstd = RS1[:, bass.ds(g * TILES + m, 1)]
                    last = dve.tensor_scalar(XN1[:, m * P:(m + 1) * P], cols(X, g, P, m * P), mean, rstd,
                                             ALU.subtract, ALU.mult)
                last.then_inc(xn1.sem, 1)

            def x1_lo(g):
                dve.wait_ge(xh1.sem, xh1.at(g))
                dve.tensor_tensor(XL1[:, :], bX[:, :], XH1[:, :].bitcast(F32), ALU.subtract).then_inc(xl1.sem, 1)

            def rotary(g, p):
                dve.wait_ge(qk.sem, qk.at(g, p + 1))
                if isinstance(g, int):
                    dve.wait_ge(tables.sem, 2 * g + p + 1)
                else:
                    dve.wait_ge(tables.sem, CHUNKS)
                if later(g):
                    dve.wait_ge(rot.sem, rot.at(g - 1, p + 1))
                cos = COS[:, bass.ds(g * 2 * QK + p * QK, QK)]
                sin = SIN[:, bass.ds(g * 2 * QK + p * QK, QK)]
                half = DK // 2
                bank = qk_bank(g, p)
                src = bank[:, :].rearrange("r (b n) -> r b n", b=2)
                dve.tensor_tensor(RA[:, p], src, cos.unsqueeze(1).to_broadcast([P, 2, QK]), ALU.mult)
                for b in range(2):
                    sw = bank[:, b * QK:(b + 1) * QK].rearrange("r (h a f) -> r h a f", a=2, f=half)[:, :, ::-1, :]
                    last = dve.tensor_tensor(RB[:, p, b].rearrange("r (h a f) -> r h a f", a=2, f=half), sw,
                                             sin.rearrange("r (h a f) -> r h a f", a=2, f=half), ALU.mult)
                last.then_inc(rparts.sem, 1)

            def rotate(g, p):
                dve.wait_ge(rparts.sem, rparts.at(g, p + 1))
                if later(g):
                    dve.wait_ge(kv.sem, kv.at(g - 1, p + 1))
                dve.tensor_tensor(QKR[:, p].rearrange("r b n -> r (b n)"), RA[:, p].rearrange("r b n -> r (b n)"),
                                  RB[:, p].rearrange("r b n -> r (b n)"), ALU.add).then_inc(rot.sem, 1)

            def masked(g, m):
                dve.wait_ge(sc_ps.sem, sc_ps.at(g, m + 1))
                if later(g):
                    dve.wait_ge(o_ps.sem, o_ps.at(g - 1, m // 2 + 1))
                elif m == 0:
                    dve.wait_ge(mask.sem, 1)
                dve.tensor_tensor(SC[:, m].rearrange("r h n -> r (h n)"), score_bank(g, m)[:, :],
                                  MASK[:, :, :].rearrange("r h n -> r (h n)"), ALU.mult).then_inc(sc_sb.sem, 1)

            def state(g, p):
                dve.wait_ge(kv.sem, kv.at(g, p + 1))
                if p == 1:
                    dve.wait_ge(o_ps.sem, o_ps.at(g, 1))
                elif later(g):
                    dve.wait_ge(o_ps.sem, o_ps.at(g - 1, 2))
                if p == 1:
                    dve.wait_ge(st.sem, st.at(g, 1))
                elif later(g):
                    dve.wait_ge(st.sem, st.at(g - 1, 2))
                else:
                    dve.wait_ge(s_zero.sem, 1)
                for h in range(H):
                    r, c = slice(h * DK, (h + 1) * DK), slice(h * DV, (h + 1) * DV)
                    last = dve.scalar_tensor_tensor(
                        out=S[r, 1 - p, :, c], in0=S[r, p, :, c], scalar=CN[r, GCH0:GCH0 + 1],
                        in1=bS[r, :].rearrange("r (b n) -> r b n", b=2)[:, :, c], op0=ALU.mult, op1=ALU.add)
                last.then_inc(st.sem, 1)

            def mean_squares(g, p):
                dve.wait_ge(sq.sem, sq.at(g, p + 1))
                dve.tensor_reduce(SS[:, p], SQ[:, p].rearrange("r (h v) -> r h v", v=DV), AX.X, ALU.add).then_inc(ss.sem, 1)
                dve.wait_ge(ss.sem, ss.at(g, p + 1))
                dve.tensor_scalar(MS[:, p], SS[:, p], 1.0 / DV, EPS, ALU.mult, ALU.add).then_inc(ms.sem, 1)

            def gate_out(g, p):
                dve.wait_ge(sq.sem, sq.at(g, p + 1))
                dve.wait_ge(sg.sem, sg.at(g, p + 1))
                if later(g):
                    dve.wait_ge(og.sem, og.at(g - 1, p + 1))
                dve.tensor_tensor(OGR[:, p], bO[:, :], SG[:, p].rearrange("r b n -> r (b n)"), ALU.mult).then_inc(ogr.sem, 1)

            def add_attention(g, p):
                dve.wait_ge(wo_ps.sem, wo_ps.at(g, p + 1))
                if later(g):
                    dve.wait_ge(kept.sem, kept.at(g - 1, p + 1))
                c = slice(p * 2 * P, (p + 1) * 2 * P)
                dve.tensor_tensor(X1[:, c], tail_bank(g, p)[:, 0:2 * P], cols(X, g, 2 * P, p * 2 * P), ALU.add).then_inc(x1.sem, 1)

            def stats2(g, p):
                dve.wait_ge(x1.sem, x1.at(g, p + 1))
                for m in (2 * p, 2 * p + 1):
                    last = dve.bn_stats(ST2[:, m, :], X1[:, m * P:(m + 1) * P])
                last.then_inc(ln2_step.sem, 1)
                dve.wait_ge(ln2_step.sem, ln2_step.at(g, 3 * p + 1))
                dve.memset(VE2[:, 2 * p:2 * p + 2], 0.0)
                for m in (2 * p, 2 * p + 1):
                    last = dve.bn_aggr(MV2[:, m, :], ST2[:, m, :])
                last.then_inc(ln2_step.sem, 1)
                dve.wait_ge(ln2_step.sem, ln2_step.at(g, 3 * p + 2))
                dve.tensor_scalar(VE2[:, 2 * p:2 * p + 2], MV2[:, 2 * p:2 * p + 2, 1], EPS, None,
                                  ALU.add).then_inc(ln2_step.sem, 1)

            def normalize2(g, p):
                dve.wait_ge(rs2.sem, rs2.at(g, p + 1))
                for m in (2 * p, 2 * p + 1):
                    last = dve.tensor_scalar(XN2[:, m * P:(m + 1) * P], X1[:, m * P:(m + 1) * P], MV2[:, m, 0:1],
                                             RS2[:, m:m + 1], ALU.subtract, ALU.mult)
                last.then_inc(xn2.sem, 1)

            def x2_lo(g, p):
                dve.wait_ge(xh2.sem, xh2.at(g, p + 1))
                c = slice(p * 2 * P, (p + 1) * 2 * P)
                dve.tensor_tensor(XL2[:, c], tail_bank(g, p)[:, 0:2 * P], XH2[:, c].bitcast(F32), ALU.subtract).then_inc(xl2.sem, 1)

            def route_a(g):
                parts = bC[:, 0:TILES * 2 * E].rearrange("r (m s e) -> r m s e", s=2, e=E)
                dve.wait_ge(logits.sem, logits.at(g))
                dve.tensor_reduce(LG[:, :, :], parts.rearrange("r m s e -> r m e s"), AX.X, ALU.add).then_inc(route.sem, 1)
                dve.wait_ge(route.sem, route.at(g, 1))
                dve.tensor_reduce(MX[:, :], LG[:, :, :], AX.X, ALU.max).then_inc(route.sem, 1)
                dve.wait_ge(route.sem, route.at(g, 2))
                dve.tensor_tensor(SHI[:, :, :], LG[:, :, :], MX[:, :].unsqueeze(2).to_broadcast([P, TILES, E]),
                                  ALU.subtract).then_inc(route.sem, 1)

            def route_b(g):
                wide = [P, TILES, E, E]
                step = [3]

                def then(ins):
                    step[0] += 1
                    ins.then_inc(route.sem, 1)
                    dve.wait_ge(route.sem, route.at(g, step[0]))

                dve.wait_ge(exped.sem, exped.at(g))
                then(dve.tensor_reduce(Z[:, :], EX[:, :, :], AX.X, ALU.add))
                then(dve.reciprocal(RZ[:, :], Z[:, :]))
                then(dve.tensor_tensor(PR[:, :, :], EX[:, :, :], RZ[:, :].unsqueeze(2).to_broadcast([P, TILES, E]), ALU.mult))
                then(dve.tensor_tensor(DIF[:, :, :, :], PR[:, :, :].unsqueeze(2).to_broadcast(wide),
                                       PR[:, :, :].unsqueeze(3).to_broadcast(wide), ALU.subtract))
                thr = CN[:, THR0:THR0 + E * E].unsqueeze(1).to_broadcast([P, TILES, E * E])
                then(dve.tensor_tensor(BEF[:, :, :, :].rearrange("r m i j -> r m (i j)"),
                                       DIF[:, :, :, :].rearrange("r m i j -> r m (i j)"), thr, ALU.is_ge))
                then(dve.tensor_reduce(RANK[:, :, :], BEF[:, :, :, :], AX.X, ALU.add))
                then(dve.scalar_tensor_tensor(out=WT[:, :, :], in0=RANK[:, :, :], scalar=float(TOP_K), in1=PR[:, :, :],
                                              op0=ALU.is_lt, op1=ALU.mult))
                then(dve.tensor_reduce(WS[:, :], WT[:, :, :], AX.X, ALU.add))
                then(dve.tensor_scalar(WSG[:, :], WS[:, :], 1e-20, None, ALU.add))
                then(dve.reciprocal(RWS[:, :], WSG[:, :]))
                then(dve.tensor_tensor(CMB[:, :, :], WT[:, :, :], RWS[:, :].unsqueeze(2).to_broadcast([P, TILES, E]), ALU.mult))
                if later(g):
                    dve.wait_ge(ct_ps.sem, ct_ps.at(g - 1))
                hi = CX[:, :, HI0:HI0 + E].bitcast(F32R)
                dve.tensor_copy(CX[:, :, HB0:HB0 + E].bitcast(F32R), CMB[:, :, :])
                then(dve.tensor_copy(hi, CMB[:, :, :]))
                dve.tensor_tensor(CX[:, :, LO0:LO0 + E], CMB[:, :, :], CX[:, :, HI0:HI0 + E],
                                  ALU.subtract).then_inc(comb.sem, 1)

            def gating(g, k):
                dve.wait_ge(spread.sem, spread.at(g, k))
                dve.wait_ge(hid.sem, hid.at(g, k + 1))
                if k >= 4:
                    dve.wait_ge(hg_lo.sem, hg_lo.at(g, k - 2))
                elif later(g):
                    dve.wait_ge(hg_lo.sem, hg_lo.at(g - 1, k + 4 if k == 3 else k + 7))
                dve.tensor_tensor(HG[:, k % 3, :], bC[:, :], HB[:, k, :], ALU.mult).then_inc(gated.sem, 1)

            def result(g):
                dve.wait_ge(yt.sem, yt.at(g))
                dve.wait_ge(kept.sem, kept.at(g, 2))
                if later(g):
                    dve.wait_ge(stored.sem, stored.at(g - 1, 32))
                dve.tensor_tensor(OUT[:, :, :].rearrange("r m n -> r (m n)"), bY[:, :], cols(X, g),
                                  ALU.add).then_inc(outs.sem, 1)

            def low_w():
                dve.wait_ge(w_hi.sem, 1)
                dve.tensor_tensor(WL[:, :], W[:, :], WH[:, :].bitcast(F32), ALU.subtract).then_inc(w_lo.sem, 1)

            def fold_norm():
                dve.wait_ge(ld_wo.sem, 16)
                dve.wait_ge(ld_gn.sem, 16)
                dve.tensor_scalar(WOG[:, :, :].rearrange("r a n -> r (a n)"), WO[:, :, :].rearrange("r a n -> r (a n)"),
                                  GN[:, 0:1], None, ALU.mult).then_inc(wog.sem, 1)

            def low_experts():
                dve.wait_ge(gw_hi.sem, 1)
                dve.tensor_tensor(GWS[:, 1, :], GW[:, :], GWS[:, 0, :].bitcast(F32), ALU.subtract).then_inc(gw_lo.sem, 1)
                dve.wait_ge(uw_hi.sem, 1)
                dve.tensor_tensor(UWL[:, :], UW[:, :], UWH[:, :].bitcast(F32), ALU.subtract).then_inc(uw_lo.sem, 1)

            def low_down():
                dve.wait_ge(dw_hi.sem, 1)
                dve.tensor_tensor(DWL[:, :], DW[:, :], DWH[:, :].bitcast(F32), ALU.subtract).then_inc(dw_lo.sem, 1)

            def low_biases():
                dve.wait_ge(db_hi.sem, 1)
                dve.tensor_tensor(DBX[HB0:P, :], DB[HB0:P, :], CT[HB0:P, 0:P].bitcast(F32),
                                  ALU.subtract).then_inc(db_lo.sem, 1)

            def selector():
                dve.wait_ge(sel_self.sem, 1)
                dve.tensor_copy(SEL[:, :, :], SELF[:, :, :]).then_inc(sel.sem, 1)

            stats1(0)
            normalize1(0)
            low_w()
            x1_lo(0)
            rotary(0, 0)
            rotate(0, 0)
            low_biases()
            stats1(1)
            rotary(0, 1)
            rotate(0, 1)
            masked(0, 0)
            masked(0, 1)
            fold_norm()
            normalize1(1)
            low_experts()
            mean_squares(0, 0)
            state(0, 0)
            gate_out(0, 0)
            x1_lo(1)
            masked(0, 2)
            masked(0, 3)
            rotary(1, 0)
            low_down()
            add_attention(0, 0)
            rotate(1, 0)
            stats2(0, 0)
            state(0, 1)
            normalize2(0, 0)
            mean_squares(0, 1)
            selector()
            gate_out(0, 1)
            masked(1, 0)
            x2_lo(0, 0)
            rotary(1, 1)
            stats1(2)
            masked(1, 1)
            add_attention(0, 1)
            stats2(0, 1)
            rotate(1, 1)
            normalize2(0, 1)
            stats1(3)
            x2_lo(0, 1)
            gate_out(1, 0)
            state(1, 0)

            def steady(g):
                f = g - 1
                route_a(f)
                mean_squares(g, 0)
                masked(g, 2)
                normalize1(g + 1)
                masked(g, 3)
                route_b(f)
                x1_lo(g + 1)
                mean_squares(g, 1)
                gate_out(g, 1)
                rotary(g + 1, 0)
                add_attention(g, 0)
                gating(f, 1)
                stats2(g, 0)
                gating(f, 2)
                normalize2(g, 0)
                rotate(g + 1, 0)
                gating(f, 3)
                x2_lo(g, 0)
                gating(f, 4)
                state(g, 1)
                gating(f, 5)
                add_attention(g, 1)
                stats2(g, 1)
                normalize2(g, 1)
                gating(f, 6)
                masked(g + 1, 0)
                gating(f, 7)
                x2_lo(g, 1)
                rotary(g + 1, 1)
                masked(g + 1, 1)
                gating(f, 8)
                rotate(g + 1, 1)
                gate_out(g + 1, 0)
                state(g + 1, 0)
                result(f)

            with dve.Fori(1, GROUPS - 1) as g:
                steady(g)
            g, f = GROUPS - 1, GROUPS - 2
            mean_squares(g, 0)
            masked(g, 2)
            route_a(f)
            masked(g, 3)
            route_b(f)
            mean_squares(g, 1)
            gate_out(g, 1)
            add_attention(g, 0)
            gating(f, 1)
            stats2(g, 0)
            gating(f, 2)
            normalize2(g, 0)
            gating(f, 3)
            x2_lo(g, 0)
            gating(f, 4)
            gating(f, 5)
            add_attention(g, 1)
            stats2(g, 1)
            gating(f, 6)
            normalize2(g, 1)
            gating(f, 7)
            x2_lo(g, 1)
            gating(f, 8)
            route_a(g)
            route_b(g)
            result(f)
            gating(g, 1)
            gating(g, 2)
            gating(g, 3)
            gating(g, 4)
            gating(g, 5)
            gating(g, 6)
            gating(g, 7)
            gating(g, 8)
            result(g)

        @block.tensor
        def _(pe):
            def keep_busy(n):
                for _ in range(n):
                    pe.matmul(bY[:, 0:P], IDN[:, :], IDN[:, :], start=True, stop=True)

            def x1_t(g):
                pe.wait_ge(xn1.sem, xn1.at(g))
                if later(g):
                    pe.wait_ge(kt.sem, kt.at(g - 1, 2))
                    pe.wait_ge(qt.sem, qt.at(g - 1, 2))
                for m in range(TILES):
                    last = pe.transpose(bX[:, m * P:(m + 1) * P], XN1[:, m * P:(m + 1) * P], IDN[:, :])
                last.then_inc(t1.sem, 1)

            def project(g, p, dst, c0, n, done):
                for b in range(2):
                    m = 2 * p + b
                    t = slice(m * P, (m + 1) * P)
                    last = product(dst[:, b * n:(b + 1) * n], (XH1[:, t], XL1[:, t]),
                                   (WH[:, c0:c0 + n], WL[:, c0:c0 + n]), True, True)
                last.then_inc(done.sem, 1)

            def proj_qk(g, p):
                if p == 0:
                    pe.wait_ge(xl1.sem, xl1.at(g))
                    if not later(g):
                        pe.wait_ge(w_lo.sem, 1)
                elif not first(g):
                    pe.wait_ge(kt.sem, kt.at(g, 1))
                    pe.wait_ge(qt.sem, qt.at(g, 1))
                project(g, p, qk_bank(g, p), 0, QK, qk)

            def proj_v(g, p):
                if p == 0:
                    pe.wait_ge(xl1.sem, xl1.at(g))
                    if later(g):
                        pe.wait_ge(xl2.sem, xl2.at(g - 1, 1 if first(g - 1) else 2))
                    else:
                        pe.wait_ge(w_lo.sem, 1)
                elif not first(g):
                    pe.wait_ge(sg.sem, sg.at(g, 1))
                project(g, p, v_bank(g, p), QK, HV, v_ps)

            def proj_g(g, p):
                if first(g) and p == 1:
                    pe.wait_ge(sg.sem, sg.at(g, 1))
                else:
                    pe.wait_ge(v_sb.sem, v_sb.at(g, p + 1))
                project(g, p, bV, QK + HV, HV, g_ps)

            def qk_t(g, p):
                pe.wait_ge(rot.sem, rot.at(g, p + 1))
                if first(g) and p == 1:
                    pe.wait_ge(kt.sem, kt.at(g, 1))
                    pe.wait_ge(qt.sem, qt.at(g, 1))
                for a in range(2):
                    for b in range(2):
                        o = (2 * a + b) * P
                        last = pe.transpose(bX[:, o:o + P], QKR[:, p, b, a * P:(a + 1) * P], IDN[:, :])
                last.then_inc(t2.sem, 1)

            def scores(g, m):
                p, b = divmod(m, 2)
                if b == 0:
                    pe.wait_ge(kt.sem, kt.at(g, p + 1))
                if first(g):
                    if m == 2:
                        pe.wait_ge(sc_sb.sem, sc_sb.at(g, 2))
                    elif m == 3:
                        pe.wait_ge(st.sem, st.at(g, 1))
                elif m in (1, 3):
                    pe.wait_ge(sc_sb.sem, sc_sb.at(g, m))
                elif m == 2:
                    pe.wait_ge(st.sem, st.at(g, 1))
                else:
                    pe.wait_ge(st.sem, st.at(g - 1, 2))
                pe.matmul(score_bank(g, m)[:, :], KT[:, p, b, :], QBD[:, p, b].rearrange("r h n -> r (h n)"), start=True,
                          stop=True).then_inc(sc_ps.sem, 1)

            def state_add(g, p):
                pe.wait_ge(sc_sb.sem, sc_sb.at(g, 1 if first(g) and p == 0 else 2 * p + 2))
                pe.wait_ge(v_sb.sem, v_sb.at(g, p + 1))
                for b in range(2):
                    last = pe.matmul(bS[:, b * HV:(b + 1) * HV], QKR[:, p, b, P:2 * P], V[:, p, b, :],
                                     start=True, stop=True)
                last.then_inc(kv.sem, 1)

            def attend(g, p):
                pe.wait_ge(qt.sem, qt.at(g, p + 1))
                if p == 1:
                    pe.wait_ge(ogr.sem, ogr.at(g, 1))
                    pe.wait_ge(st.sem, st.at(g, 1))
                elif later(g):
                    pe.wait_ge(ogr.sem, ogr.at(g - 1, 2))
                    pe.wait_ge(st.sem, st.at(g - 1, 2))
                else:
                    pe.wait_ge(s_zero.sem, 1)
                pe.wait_ge(v_sb.sem, v_sb.at(g, p + 1))
                pe.wait_ge(sc_sb.sem, sc_sb.at(g, 2 * p + 2))
                no_state = first(g) and p == 0
                for b in range(2):
                    if not no_state:
                        pe.matmul(bO[:, b * HV:(b + 1) * HV], QT[:, p, b, :], S[:, p, b, :], start=True, stop=False)
                    for h in range(H):
                        c = slice(b * HV + h * DV, b * HV + (h + 1) * DV)
                        last = pe.matmul(bO[:, c], SC[:, 2 * p + b, h, :], V[:, p, b, h * DV:(h + 1) * DV],
                                         start=no_state, stop=(no_state or h == H - 1))
                last.then_inc(o_ps.sem, 1)

            def out_t(g, p):
                pe.wait_ge(og.sem, og.at(g, p + 1))
                if p == 0:
                    pe.wait_ge(sg.sem, sg.at(g, 2))
                elif not first(g):
                    pe.wait_ge(xl2.sem, xl2.at(g, 1))
                for b in range(2):
                    for a in range(2):
                        o = (2 * b + a) * P
                        last = pe.transpose(tail_bank(g, p)[:, o:o + P], OG[:, p, o:o + P], IDN[:, :])
                last.then_inc(t3.sem, 1)

            def proj_out(g, p):
                pe.wait_ge(ogt.sem, ogt.at(g, p + 1))
                if not later(g):
                    pe.wait_ge(wog.sem, 1)
                for b in range(2):
                    for a in range(2):
                        last = pe.matmul(tail_bank(g, p)[:, b * P:(b + 1) * P], OGT[:, p, b, a, :], WOG[:, a, :],
                                         start=(a == 0), stop=(a == 1))
                last.then_inc(wo_ps.sem, 1)

            def x2_t(g, p):
                pe.wait_ge(xn2.sem, xn2.at(g, p + 1))
                for b in range(2):
                    m = 2 * p + b
                    last = pe.transpose(tail_bank(g, p)[:, b * P:(b + 1) * P], XN2[:, m * P:(m + 1) * P], IDN[:, :])
                last.then_inc(t4.sem, 1)

            def router(g):
                pe.wait_ge(xl2.sem, xl2.at(g, 2))
                if later(g):
                    pe.wait_ge(gated.sem, gated.at(g - 1, E))
                for m in range(TILES):
                    t = slice(m * P, (m + 1) * P)
                    o = m * 2 * E
                    pe.matmul(bC[:, o:o + 2 * E], XH2[:, t], GWS[:, :, :].rearrange("r s e -> r (s e)"),
                              start=True, stop=False)
                    last = pe.matmul(bC[:, o:o + E], XL2[:, t], GWS[:, 0, :], start=False, stop=True)
                last.then_inc(logits.sem, 1)

            def comb_t(g):
                pe.wait_ge(comb.sem, comb.at(g))
                for m in range(TILES):
                    last = pe.transpose(bC[:, m * P:(m + 1) * P], CX[:, m, :], IDN[:, :])
                last.then_inc(ct_ps.sem, 1)

            def up_proj(g, k):
                e = expert(k)
                if k == 0:
                    pe.wait_ge(xl2.sem, xl2.at(g, 2))
                if k >= 2:
                    pe.wait_ge(hid.sem, hid.at(g, k - 1))
                elif later(g):
                    pe.wait_ge(hid.sem, hid.at(g - 1, E + 1 - k))
                w = slice(e * P, (e + 1) * P)
                product(bU[k % 2][:, :], (UWH[:, w], UWL[:, w]), (XH2[:, :], XL2[:, :]), True, True).then_inc(up.sem, 1)

            def spread_comb(g, k):
                if k == 1:
                    pe.wait_ge(ct_sb.sem, ct_sb.at(g))
                else:
                    pe.wait_ge(gated.sem, gated.at(g, k - 1))
                pe.matmul(bC[:, :], SEL[:, expert(k), :], CT[:, :], start=True, stop=True).then_inc(spread.sem, 1)

            def down_proj(g, k):
                e = expert(k)
                pe.wait_ge(hg_lo.sem, hg_lo.at(g, k + 1))
                if k == 0:
                    if later(g):
                        pe.wait_ge(outs.sem, outs.at(g - 1))
                if k == E:
                    pe.matmul(bY[:, :], DBX[:, :], CT[:, :], start=False, stop=False)
                w = slice(e * P, (e + 1) * P)
                product(bY[:, :], (DWH[:, w], DWL[:, w]), (HGH[:, k % 3, :], HGL[:, k % 3, :]), k == 0,
                        k == E).then_inc(down.sem, 1)

            def y_t(g):
                pe.wait_ge(y_sb.sem, y_sb.at(g))
                for m in range(TILES):
                    last = pe.transpose(bY[:, m * P:(m + 1) * P], YS[:, m * P:(m + 1) * P], IDN[:, :])
                last.then_inc(yt.sem, 1)

            pe.wait_ge(idn.sem, 1)
            keep_busy(10)
            x1_t(0)
            keep_busy(4)
            proj_qk(0, 0)
            keep_busy(8)
            proj_v(0, 0)
            qk_t(0, 0)
            proj_qk(0, 1)
            proj_g(0, 0)
            proj_v(0, 1)
            scores(0, 0)
            scores(0, 1)
            qk_t(0, 1)
            attend(0, 0)
            state_add(0, 0)
            x1_t(1)
            proj_g(0, 1)
            scores(0, 2)
            scores(0, 3)
            proj_qk(1, 0)
            out_t(0, 0)
            keep_busy(1)
            state_add(0, 1)
            proj_out(0, 0)
            attend(0, 1)
            qk_t(1, 0)
            keep_busy(5)
            x2_t(0, 0)
            scores(1, 0)
            proj_qk(1, 1)
            keep_busy(1)
            scores(1, 1)
            out_t(0, 1)
            keep_busy(1)
            proj_v(1, 0)
            proj_out(0, 1)
            proj_g(1, 0)
            attend(1, 0)
            x2_t(0, 1)
            state_add(1, 0)
            pe.wait_ge(gw_lo.sem, 1)
            pe.wait_ge(uw_lo.sem, 1)
            pe.wait_ge(dw_lo.sem, 1)
            pe.wait_ge(sel.sem, 1)

            def steady(g):
                f = g - 1
                qk_t(g, 1)
                proj_v(g, 1)
                router(f)
                up_proj(f, 0)
                scores(g, 2)
                up_proj(f, 1)
                up_proj(f, 2)
                scores(g, 3)
                proj_g(g, 1)
                x1_t(g + 1)
                attend(g, 1)
                out_t(g, 0)
                up_proj(f, 3)
                up_proj(f, 4)
                proj_qk(g + 1, 0)
                comb_t(f)
                proj_out(g, 0)
                spread_comb(f, 1)
                up_proj(f, 5)
                up_proj(f, 6)
                spread_comb(f, 2)
                down_proj(f, 0)
                up_proj(f, 7)
                up_proj(f, 8)
                spread_comb(f, 3)
                x2_t(g, 0)
                state_add(g, 1)
                spread_comb(f, 4)
                qk_t(g + 1, 0)
                out_t(g, 1)
                down_proj(f, 1)
                spread_comb(f, 5)
                proj_out(g, 1)
                down_proj(f, 2)
                down_proj(f, 3)
                scores(g + 1, 0)
                spread_comb(f, 6)
                down_proj(f, 4)
                proj_qk(g + 1, 1)
                x2_t(g, 1)
                spread_comb(f, 7)
                down_proj(f, 5)
                scores(g + 1, 1)
                proj_v(g + 1, 0)
                spread_comb(f, 8)
                down_proj(f, 6)
                down_proj(f, 7)
                attend(g + 1, 0)
                proj_g(g + 1, 0)
                down_proj(f, 8)
                state_add(g + 1, 0)
                y_t(f)

            with pe.Fori(1, GROUPS - 1) as g:
                steady(g)
            g, f = GROUPS - 1, GROUPS - 2
            qk_t(g, 1)
            router(f)
            up_proj(f, 0)
            scores(g, 2)
            up_proj(f, 1)
            proj_v(g, 1)
            scores(g, 3)
            up_proj(f, 2)
            proj_g(g, 1)
            attend(g, 1)
            out_t(g, 0)
            up_proj(f, 3)
            comb_t(f)
            proj_out(g, 0)
            spread_comb(f, 1)
            up_proj(f, 4)
            up_proj(f, 5)
            spread_comb(f, 2)
            up_proj(f, 6)
            up_proj(f, 7)
            spread_comb(f, 3)
            x2_t(g, 0)
            up_proj(f, 8)
            down_proj(f, 0)
            spread_comb(f, 4)
            out_t(g, 1)
            down_proj(f, 1)
            spread_comb(f, 5)
            proj_out(g, 1)
            down_proj(f, 2)
            spread_comb(f, 6)
            down_proj(f, 3)
            spread_comb(f, 7)
            down_proj(f, 4)
            x2_t(g, 1)
            spread_comb(f, 8)
            down_proj(f, 5)
            up_proj(g, 0)
            router(g)
            down_proj(f, 6)
            down_proj(f, 7)
            up_proj(g, 1)
            up_proj(g, 2)
            down_proj(f, 8)
            up_proj(g, 3)
            up_proj(g, 4)
            y_t(f)
            comb_t(g)
            up_proj(g, 5)
            spread_comb(g, 1)
            up_proj(g, 6)
            spread_comb(g, 2)
            up_proj(g, 7)
            spread_comb(g, 3)
            down_proj(g, 0)
            spread_comb(g, 4)
            down_proj(g, 1)
            spread_comb(g, 5)
            down_proj(g, 2)
            spread_comb(g, 6)
            down_proj(g, 3)
            up_proj(g, 8)
            spread_comb(g, 7)
            down_proj(g, 4)
            spread_comb(g, 8)
            down_proj(g, 5)
            down_proj(g, 6)
            down_proj(g, 7)
            down_proj(g, 8)
            y_t(g)



def kernel(**inputs):
    import concourse.bacc as bacc
    from concourse.bass_utils import run_bass_kernel_spmd

    def arr(name):
        return np.asarray(inputs[name])

    both = np.concatenate
    feeds = {
        "x": arr("L0_attn_x"),
        "wqkvg": both([arr("L0_attn_" + n) for n in ("Wq", "Wk", "Wv", "Wg")], axis=0).T,
        "wot": arr("L0_attn_Wo").T.reshape(2, P, P).transpose(1, 0, 2),
        "gnw": np.tile(arr("L0_attn_g_norm_w"), P // DV)[:, None],
        "upw": both([arr("L0_ffn_up_w"), arr("L0_ffn_sh_up_w")[None]]).transpose(1, 0, 2).reshape(P, -1),
        "upb": both([arr("L0_ffn_up_b"), arr("L0_ffn_sh_up_b")[None]]).T,
        "dnw": both([arr("L0_ffn_down_w"), arr("L0_ffn_sh_down_w")[None]]).transpose(1, 0, 2).reshape(P, -1),
        "dnb": both([arr("L0_ffn_down_b"), arr("L0_ffn_sh_down_b")[None]]),
        "gatew": arr("L0_ffn_gate_w").T,
        "const": constants(),
    }
    feeds = {name: np.ascontiguousarray(a) for name, a in feeds.items()}
    nc = bacc.Bacc("TRN2", target_bir_lowering=False, num_devices=1)
    args = [nc.dram_tensor(name, a.shape, mybir.dt.from_np(a.dtype), kind="ExternalInput").ap()
            for name, a in feeds.items()]
    args.append(nc.dram_tensor("out", (B, T, P), F32, kind="ExternalOutput").ap())
    retention_moe_kernel(nc, *args)
    done = run_bass_kernel_spmd(nc, [feeds], core_ids=[0])
    return done.results[0]["out"]
```
